# Optimizing a Trainium2 kernel written in Bass

```python
import numpy as np
import jax
import jax.numpy as jnp

def _softmax(x, axis=-1):
    return jax.nn.softmax(x, axis=axis)

def _gelu(x):
    return jax.nn.gelu(x, approximate=True)

def _silu(x):
    return jax.nn.silu(x)

def _sigmoid(x):
    return jax.nn.sigmoid(x)

def _layernorm(x, axis=-1, eps=1e-05):
    m = jnp.mean(x, axis=axis, keepdims=True)
    v = jnp.var(x, axis=axis, keepdims=True)
    return (x - m) / jnp.sqrt(v + eps)

def _scatter_add(tgt, idx, src, axis=0):
    return tgt.at[idx].add(src)

def _segment_sum(src, seg, n):
    return jax.ops.segment_sum(src, seg, n)
kernel_name = 'mk_vit_tower_d1_tok_img256_r4_bc3f97'

def setup_inputs(seed: int=0):
    np.random.seed(seed)
    _w = jnp.asarray

    def _rec_inputs():
        import jax
        import jax.numpy as jnp
        _rk = jax.random.key(seed)
        x = -0.00040386 + 0.999972 * jax.random.normal(jax.random.fold_in(_rk, 1), (16, 3, 224, 224), jnp.float32)
        return x
    x = _rec_inputs()

    def _L0_tok_setup():
        import jax, jax.numpy as jnp
        import numpy as np
        EPS = 1e-05
        P = 8
        DIM = 64
        NUM_TOKENS = 64
        PATCH_DIM = 3 * P * P

        def layernorm(x, g, b):
            mu = jnp.mean(x, axis=-1, keepdims=True)
            var = jnp.mean(jnp.square(x - mu), axis=-1, keepdims=True)
            return (x - mu) * jax.lax.rsqrt(var + EPS) * g + b
        key = jax.random.key(seed)
        ks = jax.random.split(key, 8)
        b, c, h, w = (16, 3, 128, 128)
        x = jax.random.normal(ks[0], (b, c, h, w), dtype=jnp.float32)
        ln1_g = jnp.ones((PATCH_DIM,), jnp.float32)
        ln1_b = jnp.zeros((PATCH_DIM,), jnp.float32)
        W1 = jax.random.normal(ks[1], (PATCH_DIM, DIM), jnp.float32) * 0.02
        b1 = jnp.zeros((DIM,), jnp.float32)
        ln2_g = jnp.ones((DIM,), jnp.float32)
        ln2_b = jnp.zeros((DIM,), jnp.float32)
        Wp1 = jax.random.normal(ks[2], (DIM, DIM), jnp.float32) * 0.02
        bp1 = jnp.zeros((DIM,), jnp.float32)
        lnp_g = jnp.ones((DIM,), jnp.float32)
        lnp_b = jnp.zeros((DIM,), jnp.float32)
        Wp2 = jax.random.normal(ks[3], (DIM, NUM_TOKENS), jnp.float32) * 0.02
        bp2 = jnp.zeros((NUM_TOKENS,), jnp.float32)
        return {'x': x, 'ln1_g': ln1_g, 'ln1_b': ln1_b, 'W1': W1, 'b1': b1, 'ln2_g': ln2_g, 'ln2_b': ln2_b, 'Wp1': Wp1, 'bp1': bp1, 'lnp_g': lnp_g, 'lnp_b': lnp_b, 'Wp2': Wp2, 'bp2': bp2}
    _L0_tok_all = _L0_tok_setup()
    _L0_tok_in = {k: v for k, v in _L0_tok_all.items() if k in ('ln1_g', 'ln1_b', 'W1', 'b1', 'ln2_g', 'ln2_b', 'Wp1', 'bp1', 'lnp_g', 'lnp_b', 'Wp2', 'bp2')}
    del _L0_tok_all

    def _L0_attn_setup():
        import jax, jax.numpy as jnp
        import numpy as np
        D_MODEL = 64
        D_STATE = 16
        DT_RANK = 16
        D_CONV = 2

        def _mamba_params(key, prefix):
            ks = jax.random.split(key, 6)
            D, N, R = (D_MODEL, D_STATE, DT_RANK)
            s = 0.02
            p = {prefix + 'in_w': jax.random.normal(ks[0], (2 * D, D), jnp.float32) * s, prefix + 'conv_w': jax.random.normal(ks[1], (D, D_CONV), jnp.float32) * s, prefix + 'conv_b': jnp.zeros((D,), jnp.float32), prefix + 'xproj_w': jax.random.normal(ks[2], (R + 2 * N, D), jnp.float32) * s, prefix + 'dt_w': jax.random.normal(ks[3], (D, R), jnp.float32) * s, prefix + 'dt_b': jnp.full((D,), -4.6, jnp.float32), prefix + 'A_log': jnp.log(jnp.tile(jnp.arange(1, N + 1, dtype=jnp.float32), (D, 1))), prefix + 'D': jnp.ones((D,), jnp.float32), prefix + 'out_w': jax.random.normal(ks[4], (D, D), jnp.float32) * s}
            return p

        def _mamba(x, in_w, conv_w, conv_b, xproj_w, dt_w, dt_b, A_log, Dp, out_w):
            B, L, D = x.shape
            N = A_log.shape[1]
            R = dt_w.shape[1]
            xz = jnp.einsum('bld,ed->ble', x, in_w)
            xc, z = jnp.split(xz, 2, axis=-1)
            xprev = jnp.pad(xc, ((0, 0), (1, 0), (0, 0)))[:, :-1]
            xc = jax.nn.silu(xprev * conv_w[:, 0] + xc * conv_w[:, 1] + conv_b)
            dbc = jnp.einsum('bld,ed->ble', xc, xproj_w)
            dt = jax.nn.softplus(jnp.einsum('blr,dr->bld', dbc[..., :R], dt_w) + dt_b)
            Bm = dbc[..., R:R + N]
            Cm = dbc[..., R + N:]
            A = -jnp.exp(A_log)
            dA = jnp.exp(dt[..., None] * A)
            dBx = dt[..., None] * Bm[:, :, None, :] * xc[..., None]

            def step(h, inp):
                a, bx, c = inp
                h = a * h + bx
                y = jnp.einsum('bdn,bn->bd', h, c)
                return (h, y)
            h0 = jnp.zeros((B, D, N), x.dtype)
            _, ys = jax.lax.scan(step, h0, (dA.transpose(1, 0, 2, 3), dBx.transpose(1, 0, 2, 3), Cm.transpose(1, 0, 2)))
            y = ys.transpose(1, 0, 2) + Dp * xc
            y = y * jax.nn.silu(z)
            return jnp.einsum('bld,ed->ble', y, out_w)
        key = jax.random.key(seed)
        kx, kf, kr = jax.random.split(key, 3)
        inp = {'x': jax.random.normal(kx, (4, 512, D_MODEL), jnp.float32)}
        inp.update(_mamba_params(kf, 'f_'))
        inp.update(_mamba_params(kr, 'r_'))
        return inp
    _L0_attn_all = _L0_attn_setup()
    _L0_attn_in = {k: v for k, v in _L0_attn_all.items() if k in ('f_in_w', 'f_conv_w', 'f_conv_b', 'f_xproj_w', 'f_dt_w', 'f_dt_b', 'f_A_log', 'f_D', 'f_out_w', 'r_in_w', 'r_conv_w', 'r_conv_b', 'r_xproj_w', 'r_dt_w', 'r_dt_b', 'r_A_log', 'r_D', 'r_out_w')}
    del _L0_attn_all

    def _L0_ffn_setup():
        import jax, jax.numpy as jnp
        import numpy as np
        NUM_EXPERTS = 8
        TOP_K = 2
        B, S, D = (8, 2048, 64)

        def _moe(tokens, router_w, w1, b1, w2, b2):
            N = tokens.shape[0]
            E = router_w.shape[0]
            logits = tokens.astype(jnp.float32) @ router_w.astype(jnp.float32).T
            probs = jax.nn.softmax(logits, axis=-1)
            rw, re = jax.lax.top_k(probs, TOP_K)
            if TOP_K > 1:
                rw = rw / jnp.maximum(rw.sum(-1, keepdims=True), 1e-12)
            rw = rw.astype(tokens.dtype)
            combine = jnp.zeros((N, E), tokens.dtype).at[jnp.arange(N)[:, None], re].set(rw)
            out = tokens
            for e in range(E):
                h = jax.nn.gelu(tokens @ w1[e] + b1[e], approximate=False)
                y = h @ w2[e] + b2[e]
                out = out + combine[:, e:e + 1] * y
            return out
        key = jax.random.key(seed)
        ks = jax.random.split(key, 4)
        scale = 1.0 / np.sqrt(D).astype(np.float32)
        return {'input_embeddings': jax.random.normal(ks[0], (B, S, D), jnp.float32), 'router_w': jax.random.normal(ks[1], (NUM_EXPERTS, D), jnp.float32) * scale, 'w1': jax.random.normal(ks[2], (NUM_EXPERTS, D, D), jnp.float32) * scale, 'b1': jnp.zeros((NUM_EXPERTS, D), jnp.float32), 'w2': jax.random.normal(ks[3], (NUM_EXPERTS, D, D), jnp.float32) * scale, 'b2': jnp.zeros((NUM_EXPERTS, D), jnp.float32)}
    _L0_ffn_all = _L0_ffn_setup()
    _L0_ffn_in = {k: v for k, v in _L0_ffn_all.items() if k in ('router_w', 'w1', 'b1', 'w2', 'b2')}
    del _L0_ffn_all
    return {'x': x, 'L0_tok_ln1_g': _L0_tok_in['ln1_g'], 'L0_tok_ln1_b': _L0_tok_in['ln1_b'], 'L0_tok_W1': _L0_tok_in['W1'], 'L0_tok_b1': _L0_tok_in['b1'], 'L0_tok_ln2_g': _L0_tok_in['ln2_g'], 'L0_tok_ln2_b': _L0_tok_in['ln2_b'], 'L0_tok_Wp1': _L0_tok_in['Wp1'], 'L0_tok_bp1': _L0_tok_in['bp1'], 'L0_tok_lnp_g': _L0_tok_in['lnp_g'], 'L0_tok_lnp_b': _L0_tok_in['lnp_b'], 'L0_tok_Wp2': _L0_tok_in['Wp2'], 'L0_tok_bp2': _L0_tok_in['bp2'], 'L0_attn_f_in_w': _L0_attn_in['f_in_w'], 'L0_attn_f_conv_w': _L0_attn_in['f_conv_w'], 'L0_attn_f_conv_b': _L0_attn_in['f_conv_b'], 'L0_attn_f_xproj_w': _L0_attn_in['f_xproj_w'], 'L0_attn_f_dt_w': _L0_attn_in['f_dt_w'], 'L0_attn_f_dt_b': _L0_attn_in['f_dt_b'], 'L0_attn_f_A_log': _L0_attn_in['f_A_log'], 'L0_attn_f_D': _L0_attn_in['f_D'], 'L0_attn_f_out_w': _L0_attn_in['f_out_w'], 'L0_attn_r_in_w': _L0_attn_in['r_in_w'], 'L0_attn_r_conv_w': _L0_attn_in['r_conv_w'], 'L0_attn_r_conv_b': _L0_attn_in['r_conv_b'], 'L0_attn_r_xproj_w': _L0_attn_in['r_xproj_w'], 'L0_attn_r_dt_w': _L0_attn_in['r_dt_w'], 'L0_attn_r_dt_b': _L0_attn_in['r_dt_b'], 'L0_attn_r_A_log': _L0_attn_in['r_A_log'], 'L0_attn_r_D': _L0_attn_in['r_D'], 'L0_attn_r_out_w': _L0_attn_in['r_out_w'], 'L0_ffn_router_w': _L0_ffn_in['router_w'], 'L0_ffn_w1': _L0_ffn_in['w1'], 'L0_ffn_b1': _L0_ffn_in['b1'], 'L0_ffn_w2': _L0_ffn_in['w2'], 'L0_ffn_b2': _L0_ffn_in['b2']}

def reference(x, L0_tok_ln1_g, L0_tok_ln1_b, L0_tok_W1, L0_tok_b1, L0_tok_ln2_g, L0_tok_ln2_b, L0_tok_Wp1, L0_tok_bp1, L0_tok_lnp_g, L0_tok_lnp_b, L0_tok_Wp2, L0_tok_bp2, L0_attn_f_in_w, L0_attn_f_conv_w, L0_attn_f_conv_b, L0_attn_f_xproj_w, L0_attn_f_dt_w, L0_attn_f_dt_b, L0_attn_f_A_log, L0_attn_f_D, L0_attn_f_out_w, L0_attn_r_in_w, L0_attn_r_conv_w, L0_attn_r_conv_b, L0_attn_r_xproj_w, L0_attn_r_dt_w, L0_attn_r_dt_b, L0_attn_r_A_log, L0_attn_r_D, L0_attn_r_out_w, L0_ffn_router_w, L0_ffn_w1, L0_ffn_b1, L0_ffn_w2, L0_ffn_b2):
    import jax
    import jax.numpy as jnp

    def _L0_tok_ref(x, ln1_g, ln1_b, W1, b1, ln2_g, ln2_b, Wp1, bp1, lnp_g, lnp_b, Wp2, bp2):
        import jax, jax.numpy as jnp
        import numpy as np
        EPS = 1e-05
        P = 8
        DIM = 64
        NUM_TOKENS = 64
        PATCH_DIM = 3 * P * P

        def layernorm(x, g, b):
            mu = jnp.mean(x, axis=-1, keepdims=True)
            var = jnp.mean(jnp.square(x - mu), axis=-1, keepdims=True)
            return (x - mu) * jax.lax.rsqrt(var + EPS) * g + b
        b, c, H, W = x.shape
        hp, wp = (H // P, W // P)
        patches = x.reshape(b, c, hp, P, wp, P)
        patches = jnp.transpose(patches, (0, 2, 4, 3, 5, 1))
        patches = patches.reshape(b, hp * wp, P * P * c)
        tokens = layernorm(patches, ln1_g, ln1_b)
        tokens = tokens @ W1 + b1
        tokens = layernorm(tokens, ln2_g, ln2_b)
        q = tokens
        k = tokens
        tokens = jnp.concatenate([q, k, tokens], axis=1)
        h1 = layernorm(tokens @ Wp1 + bp1, lnp_g, lnp_b)
        h1 = jax.nn.silu(h1)
        return h1 @ Wp2 + bp2

    def _L0_attn_ref(x, f_in_w, f_conv_w, f_conv_b, f_xproj_w, f_dt_w, f_dt_b, f_A_log, f_D, f_out_w, r_in_w, r_conv_w, r_conv_b, r_xproj_w, r_dt_w, r_dt_b, r_A_log, r_D, r_out_w):
        import jax, jax.numpy as jnp
        import numpy as np
        D_MODEL = 64
        D_STATE = 16
        DT_RANK = 16
        D_CONV = 2

        def _mamba_params(key, prefix):
            ks = jax.random.split(key, 6)
            D, N, R = (D_MODEL, D_STATE, DT_RANK)
            s = 0.02
            p = {prefix + 'in_w': jax.random.normal(ks[0], (2 * D, D), jnp.float32) * s, prefix + 'conv_w': jax.random.normal(ks[1], (D, D_CONV), jnp.float32) * s, prefix + 'conv_b': jnp.zeros((D,), jnp.float32), prefix + 'xproj_w': jax.random.normal(ks[2], (R + 2 * N, D), jnp.float32) * s, prefix + 'dt_w': jax.random.normal(ks[3], (D, R), jnp.float32) * s, prefix + 'dt_b': jnp.full((D,), -4.6, jnp.float32), prefix + 'A_log': jnp.log(jnp.tile(jnp.arange(1, N + 1, dtype=jnp.float32), (D, 1))), prefix + 'D': jnp.ones((D,), jnp.float32), prefix + 'out_w': jax.random.normal(ks[4], (D, D), jnp.float32) * s}
            return p

        def _mamba(x, in_w, conv_w, conv_b, xproj_w, dt_w, dt_b, A_log, Dp, out_w):
            B, L, D = x.shape
            N = A_log.shape[1]
            R = dt_w.shape[1]
            xz = jnp.einsum('bld,ed->ble', x, in_w)
            xc, z = jnp.split(xz, 2, axis=-1)
            xprev = jnp.pad(xc, ((0, 0), (1, 0), (0, 0)))[:, :-1]
            xc = jax.nn.silu(xprev * conv_w[:, 0] + xc * conv_w[:, 1] + conv_b)
            dbc = jnp.einsum('bld,ed->ble', xc, xproj_w)
            dt = jax.nn.softplus(jnp.einsum('blr,dr->bld', dbc[..., :R], dt_w) + dt_b)
            Bm = dbc[..., R:R + N]
            Cm = dbc[..., R + N:]
            A = -jnp.exp(A_log)
            dA = jnp.exp(dt[..., None] * A)
            dBx = dt[..., None] * Bm[:, :, None, :] * xc[..., None]

            def step(h, inp):
                a, bx, c = inp
                h = a * h + bx
                y = jnp.einsum('bdn,bn->bd', h, c)
                return (h, y)
            h0 = jnp.zeros((B, D, N), x.dtype)
            _, ys = jax.lax.scan(step, h0, (dA.transpose(1, 0, 2, 3), dBx.transpose(1, 0, 2, 3), Cm.transpose(1, 0, 2)))
            y = ys.transpose(1, 0, 2) + Dp * xc
            y = y * jax.nn.silu(z)
            return jnp.einsum('bld,ed->ble', y, out_w)
        fwd = _mamba(x, f_in_w, f_conv_w, f_conv_b, f_xproj_w, f_dt_w, f_dt_b, f_A_log, f_D, f_out_w)
        x_flip = jnp.flip(x, axis=1)
        bwd = _mamba(x_flip, r_in_w, r_conv_w, r_conv_b, r_xproj_w, r_dt_w, r_dt_b, r_A_log, r_D, r_out_w)
        return fwd + jnp.flip(bwd, axis=1)

    def _L0_ffn_ref(input_embeddings, router_w, w1, b1, w2, b2):
        import jax, jax.numpy as jnp
        import numpy as np
        NUM_EXPERTS = 8
        TOP_K = 2
        B, S, D = (8, 2048, 64)

        def _moe(tokens, router_w, w1, b1, w2, b2):
            N = tokens.shape[0]
            E = router_w.shape[0]
            logits = tokens.astype(jnp.float32) @ router_w.astype(jnp.float32).T
            probs = jax.nn.softmax(logits, axis=-1)
            rw, re = jax.lax.top_k(probs, TOP_K)
            if TOP_K > 1:
                rw = rw / jnp.maximum(rw.sum(-1, keepdims=True), 1e-12)
            rw = rw.astype(tokens.dtype)
            combine = jnp.zeros((N, E), tokens.dtype).at[jnp.arange(N)[:, None], re].set(rw)
            out = tokens
            for e in range(E):
                h = jax.nn.gelu(tokens @ w1[e] + b1[e], approximate=False)
                y = h @ w2[e] + b2[e]
                out = out + combine[:, e:e + 1] * y
            return out
        b, s, d = input_embeddings.shape
        tokens = input_embeddings.reshape(b * s, d)
        return _moe(tokens, router_w, w1, b1, w2, b2).reshape(b, s, d)
    h = _L0_tok_ref(x, L0_tok_ln1_g, L0_tok_ln1_b, L0_tok_W1, L0_tok_b1, L0_tok_ln2_g, L0_tok_ln2_b, L0_tok_Wp1, L0_tok_bp1, L0_tok_lnp_g, L0_tok_lnp_b, L0_tok_Wp2, L0_tok_bp2)
    h = h + _L0_attn_ref(_layernorm(h, axis=-1), L0_attn_f_in_w, L0_attn_f_conv_w, L0_attn_f_conv_b, L0_attn_f_xproj_w, L0_attn_f_dt_w, L0_attn_f_dt_b, L0_attn_f_A_log, L0_attn_f_D, L0_attn_f_out_w, L0_attn_r_in_w, L0_attn_r_conv_w, L0_attn_r_conv_b, L0_attn_r_xproj_w, L0_attn_r_dt_w, L0_attn_r_dt_b, L0_attn_r_A_log, L0_attn_r_D, L0_attn_r_out_w)
    h = h + _L0_ffn_ref(_layernorm(h, axis=-1), L0_ffn_router_w, L0_ffn_w1, L0_ffn_b1, L0_ffn_w2, L0_ffn_b2)
    return h

_drawn_inputs = setup_inputs


def setup_inputs(seed=0):
    import zlib

    import numpy as np

    out = dict(_drawn_inputs(seed))
    spreads = {'L0_tok_ln1_g': (1.0, 0.2),
     'L0_tok_ln1_b': (0.0, 0.1),
     'L0_tok_b1': (0.0, 0.1),
     'L0_tok_ln2_g': (1.0, 0.2),
     'L0_tok_ln2_b': (0.0, 0.1),
     'L0_tok_bp1': (0.0, 0.1),
     'L0_tok_lnp_g': (1.0, 0.2),
     'L0_tok_lnp_b': (0.0, 0.1),
     'L0_tok_bp2': (0.0, 0.1),
     'L0_attn_f_conv_b': (0.0, 0.678),
     'L0_attn_f_dt_b': (-4.599999904632568, 0.6),
     'L0_attn_f_D': (1.0, 0.6),
     'L0_attn_r_conv_b': (0.0, 0.8),
     'L0_attn_r_dt_b': (-4.599999904632568, 0.6),
     'L0_attn_r_D': (1.0, 0.6),
     'L0_ffn_b1': (0.0, 0.1),
     'L0_ffn_b2': (0.0, 0.1)}
    factors = {'L0_attn_f_in_w': 6.296,
     'L0_attn_f_conv_w': 8.0,
     'L0_attn_f_xproj_w': 8.0,
     'L0_attn_f_dt_w': 24.122,
     'L0_attn_f_A_log': 8.0,
     'L0_attn_f_out_w': 7.588,
     'L0_attn_r_in_w': 6.3,
     'L0_attn_r_conv_w': 8.0,
     'L0_attn_r_xproj_w': 8.0,
     'L0_attn_r_dt_w': 8.0,
     'L0_attn_r_A_log': 8.0,
     'L0_attn_r_out_w': 7.094}
    for name, (base, spread) in spreads.items():
        noise = np.random.default_rng([zlib.crc32(name.encode()), seed]).standard_normal(out[name].shape)
        drawn = base * np.exp(spread * noise) if base else spread * noise
        out[name] = jnp.asarray(drawn.astype(out[name].dtype))
    for name, factor in factors.items():
        out[name] = (out[name] * factor).astype(out[name].dtype)
    return out
```

```python
import numpy as np

import concourse.bass as bass
from concourse import mybir
from contextlib import ExitStack

F32 = mybir.dt.float32
BF16 = mybir.dt.bfloat16
ALU = mybir.AluOpType
ACT = mybir.ActivationFunctionType
AX_X = mybir.AxisListType.X

B, CH, IMG, PATCH = 16, 3, 224, 8
D = 64
NT = (IMG // PATCH) ** 2
COPIES = 3
L = COPIES * NT
NF = CH * PATCH * PATCH
NS = 16
NR = 16
NE = 8
EPS = 1e-5
PAIRS = B // 2
KF = NF // 2
HT = NT // 2
TC = NT + 1
TP = TC + 1
TH = TP // 2
DB = 8
NJ = D // DB
TILES = 2 * NJ
QJ = 4
NQ = TILES // QJ
CK = 294
NCK = L // CK
TT = 98
NTT = CK // TT

PACK = [
    ("w1T", D, 2 * KF), ("w1dup", KF, 2 * 128), ("ln1g", KF, 2), ("ln1b", KF, 2),
    ("b1", 128, 1), ("g2", 128, 1), ("be2", 128, 1), ("bp1", 128, 1), ("gp", 128, 1), ("bep", 128, 1), ("bp2", 128, 1),
    ("wp1", 128, 128), ("wp1T", 128, 128), ("wp2", 128, 128), ("wp2T", 128, 128),
    ("cen", 128, 128), ("avg", 128, 128), ("ones1", KF, KF),
    ("inx", 128, 2 * D), ("convw", 128, 2 * D), ("inz", 128, 2 * D),
    ("convb", 128, 1), ("dtb", 128, 1), ("dvec", 128, 1), ("wbc", 128, 2 * 128),
    ("wdtr", 128, 32), ("wdt", 32, 128), ("alog", 128, TILES),
    ("ysel", 128, QJ * 32), ("mask8", 128, DB), ("wout", 128, 2 * D),
    ("router", 128, 2 * NE), ("ew1", 128, 4 * 128), ("eb1", 128, 4), ("ew2", 128, 4 * D), ("eb2", 16, 2 * D),
    ("rank", TT, NTT * 2 * NE), ("ident", TT, TT),
    ("selbc", 96, QJ * 128), ("selcb", 80, 8 * 128),
]
AT, NW = {}, 0
for _name, _rows, _cols in PACK:
    AT[_name] = (NW, _rows, _cols)
    NW += _cols


def vit_tower(nc, x, wpack, out):
    with ExitStack() as top:
        def sem(name):
            return top.enter_context(nc.semaphore(name))

        ps = top.enter_context(nc.psum_tensor("ps", [128, 8, 512], F32))
        wsb = top.enter_context(nc.sbuf_tensor("wsb", [128, NW], F32))
        h_d = nc.dram_tensor("h_d", (PAIRS + 1, 128, NT), F32, kind="Internal").ap()
        hn_d = nc.dram_tensor("hn_d", (PAIRS + 1, 128, TP), F32, kind="Internal").ap()
        h2_d = nc.dram_tensor("h2_d", (PAIRS + 2, 128, L), F32, kind="Internal").ap()

        def w(name):
            at, rows, cols = AT[name]
            return wsb[0:rows, at:at + cols]

        def w3(name, n):
            return w(name).rearrange("p (a b) -> p a b", a=n)

        w1c = top.enter_context(nc.sbuf_tensor("w1c", [KF, 2, D], F32))
        wp1g = top.enter_context(nc.sbuf_tensor("wp1g", [128, 128], F32))
        wp2c = top.enter_context(nc.sbuf_tensor("wp2c", [128, 128], F32))
        vecs = top.enter_context(nc.sbuf_tensor("vecs", [128, 8], F32))
        c0c, bp1c, bp2c = vecs[:, 0:1], vecs[:, 1:2], vecs[:, 2:3]
        v_c0, v_bp1, v_eps = vecs[:, 3:4], vecs[:, 4:5], vecs[:, 5:6]
        wconv = top.enter_context(nc.sbuf_tensor("wconv", [128, 2, D], F32))
        aneg = top.enter_context(nc.sbuf_tensor("aneg", [128, TILES], F32))
        selbc = top.enter_context(nc.sbuf_tensor("selbc", [96, QJ, 128], BF16))
        selcb = top.enter_context(nc.sbuf_tensor("selcb", [80, 8, 128], BF16))

        tokenize(nc, ps, sem, w, w3, x, wpack, wsb, h_d, hn_d, h2_d, w1c, wp1g, wp2c,
                 (c0c, bp1c, bp2c, v_c0, v_bp1, v_eps), wconv, aneg, selbc, selcb)
        mamba(nc, ps, sem, w, w3, h_d, hn_d, h2_d, wconv, aneg, selbc)
        experts(nc, ps, sem, w, w3, h2_d, out, selcb, v_eps)


def tokenize(nc, ps, sem, w, w3, x, wpack, wsb, h_d, hn_d, h2_d, w1c, wp1g, wp2c, cols, wconv, aneg, selbc, selcb):
    c0c, bp1c, bp2c, v_c0, v_bp1, v_eps = cols
    with ExitStack() as ctx:
        def sb(name, shape, dt=F32):
            return ctx.enter_context(nc.sbuf_tensor(name, shape, dt))

        zero = sb("zero", [128, L])
        w1g = sb("w1g", [KF, 2, D])
        xin = [sb(f"xin{h}", [KF, 2, 2 * HT]) for h in range(2)]
        xsq = [sb(f"xsq{h}", [KF, 2, 2 * HT]) for h in range(2)]
        xsum = [sb(f"xsum{h}", [KF, 2 * HT]) for h in range(2)]
        qsum = [sb(f"qsum{h}", [KF, 2 * HT]) for h in range(2)]
        unit = {n: [sb(f"{n}{h}", [128, HT]) for h in range(2)] for n in
                ("musq", "var1", "sd1", "rs1", "yc", "sq2", "sd2", "rs2", "tok", "sq3", "sd3", "rs3", "t3", "act",
                 "hs", "sq4", "sd4", "rs4")}
        hns = sb("hns", [128, TP])
        wload, zeroed, zstored = sem("wload"), sem("zeroed"), sem("zstored")
        su_pe, su_act, su_dve, w_ready = sem("su_pe"), sem("su_act"), sem("su_dve"), sem("w_ready")
        S = {n: [sem(f"t_{n}{h}") for h in range(2)] for n in
             ("x_in", "xsq", "sums", "a_mm", "stat_mm", "musq", "var1", "sd1", "rs1", "yc", "sq2", "var2_mm", "sd2",
              "rs2", "tok", "u_mm", "sq3", "var3_mm", "sd3", "rs3", "t3", "act", "h_mm", "hs", "sq4", "var4_mm",
              "sd4", "rs4", "hns", "h_out", "hn_out", "ends")}
        bank = lambda h, k: ps[:, 4 * h + k, 0:HT]
        BY = {n: 16 if n in ("x_in", "h_out", "hn_out") else 1 for n in S}
        done = lambda i: i + 2
        last = lambda i: i + 1

        def images(h):
            return [(slice(64 * im, 64 * im + 64), slice(HT * im, HT * im + HT)) for im in range(2)]

        block = ctx.enter_context(nc.Block())

        @block.gpsimd
        def _(pool):
            for n in S:
                for h in range(2):
                    pool.sem_inc(S[n][h], BY[n])

        @block.sync
        def _(sp):
            sp.dma_start(wsb[:, :], wpack).then_inc(wload, 16)
            sp.wait_ge(zeroed, 1)
            sp.dma_start(h_d[0], zero[:, 0:NT]).then_inc(zstored, 16)
            sp.dma_start(hn_d[PAIRS], zero[:, 0:TP]).then_inc(zstored, 16)
            sp.dma_start(h2_d[PAIRS + 1], zero[:, :]).then_inc(zstored, 16)
            with sp.Fori(0, PAIRS) as i:
                for h in range(2):
                    sp.wait_ge(S["a_mm"][h], last(i))
                    sp.wait_ge(S["xsq"][h], last(i))
                    sp.wait_ge(S["sums"][h], last(i))
                    sp.dma_start(xin[h][:, :, :], x[i, h]).then_inc(S["x_in"][h], 16)
                for h in range(2):
                    sp.wait_ge(S["hs"][h], done(i))
                    sp.dma_start(h_d[i + 1, :, HT * h:HT * h + HT], unit["hs"][h][:, :]).then_inc(S["h_out"][h], 16)
                sp.wait_ge(S["ends"][0], done(i))
                sp.dma_start(hn_d[i], hns[:, :]).then_inc(S["hn_out"][0], 16)
            sp.wait_ge(zstored, 48)
            for h in range(2):
                sp.wait_ge(S["h_out"][h], 16 * done(PAIRS - 1))
            sp.wait_ge(S["hn_out"][0], 16 * done(PAIRS - 1))

        @block.tensor
        def _(pe):
            pe.wait_ge(wload, 16)
            for c in range(2):
                nc.tensor.matmul(ps[0:KF, c, 0:D], w3("w1T", 2)[:, c, :], w("cen")[0:D, 0:D],
                                 start=True, stop=True).then_inc(su_pe, 1)
            nc.tensor.matmul(ps[:, 2, 0:128], w("wp1T"), w("cen"), start=True, stop=True).then_inc(su_pe, 1)
            nc.tensor.matmul(ps[:, 3, 0:128], w("wp2T"), w("cen"), start=True, stop=True).then_inc(su_pe, 1)
            for c in range(2):
                mm = nc.tensor.matmul(ps[:, 4, 0:1], w3("w1dup", 2)[:, c, :], w3("ln1b", 2)[:, c, :],
                                      start=(c == 0), stop=(c == 1))
            mm.then_inc(su_pe, 1)
            nc.tensor.matmul(ps[:, 5, 0:1], w("wp1"), w("be2"), start=True, stop=True).then_inc(su_pe, 1)
            pe.wait_ge(su_dve, 2)
            for c in range(2):
                mm = nc.tensor.matmul(ps[0:KF, 6, 0:D], w("ones1"), w1g[:, c, :], start=(c == 0), stop=(c == 1))
            mm.then_inc(su_pe, 1)
            pe.wait_ge(su_dve, 5)
            nc.tensor.matmul(ps[:, 7, 0:1], w("cen"), v_c0, start=True, stop=True).then_inc(su_pe, 1)
            nc.tensor.matmul(ps[:, 4, 0:1], w("cen"), v_bp1, start=True, stop=True).then_inc(su_pe, 1)
            nc.tensor.matmul(ps[:, 5, 0:1], w("cen"), w("bp2"), start=True, stop=True).then_inc(su_pe, 1)
            pe.wait_ge(w_ready, 1)
            with pe.Fori(0, PAIRS) as i:
                for h in range(2):
                    pe.wait_ge(S["x_in"][h], 16 * done(i))
                    pe.wait_ge(S["hns"][h], last(i))
                    for im, (rows, toks) in enumerate(images(h)):
                        for c in range(2):
                            mm = nc.tensor.matmul(bank(h, 0)[rows, :], w1c[:, c, :], xin[h][:, c, toks],
                                                  start=(c == 0), stop=(c == 1))
                    mm.then_inc(S["a_mm"][h], 1)
                    pe.wait_ge(S["sums"][h], done(i))
                    pe.wait_ge(S["sd4"][h], last(i))
                    pe.wait_ge(S["hs"][h], last(i))
                    for k, s in ((1, xsum), (2, qsum)):
                        for rows, toks in images(h):
                            mm = nc.tensor.matmul(bank(h, k)[rows, :], w("ones1")[:, 0:D], s[h][:, toks],
                                                  start=True, stop=True)
                    mm.then_inc(S["stat_mm"][h], 1)
                for h in range(2):
                    pe.wait_ge(S["sq2"][h], done(i))
                    nc.tensor.matmul(bank(h, 1), w("avg"), unit["sq2"][h][:, :], start=True, stop=True)\
                        .then_inc(S["var2_mm"][h], 1)
                for h in range(2):
                    pe.wait_ge(S["tok"][h], done(i))
                    nc.tensor.matmul(bank(h, 0), wp1g[:, :], unit["tok"][h][:, :], start=True, stop=True)\
                        .then_inc(S["u_mm"][h], 1)
                for h in range(2):
                    pe.wait_ge(S["sq3"][h], done(i))
                    pe.wait_ge(S["sd2"][h], done(i))
                    nc.tensor.matmul(bank(h, 1), w("avg"), unit["sq3"][h][:, :], start=True, stop=True)\
                        .then_inc(S["var3_mm"][h], 1)
                for h in range(2):
                    pe.wait_ge(S["act"][h], done(i))
                    pe.wait_ge(S["t3"][h], done(i))
                    nc.tensor.matmul(bank(h, 0), wp2c[:, :], unit["act"][h][:, :], start=True, stop=True)
                    nc.tensor.matmul(bank(h, 2), w("wp2"), unit["act"][h][:, :], start=True, stop=True)\
                        .then_inc(S["h_mm"][h], 1)
                for h in range(2):
                    pe.wait_ge(S["sq4"][h], done(i))
                    pe.wait_ge(S["sd3"][h], done(i))
                    nc.tensor.matmul(bank(h, 1), w("avg"), unit["sq4"][h][:, :], start=True, stop=True)\
                        .then_inc(S["var4_mm"][h], 1)

        @block.scalar
        def _(act):
            act.wait_ge(wload, 16)
            nc.scalar.activation(aneg[:, :], w("alog"), ACT.Exp).then_inc(su_act, 1)
            act.wait_ge(w_ready, 1)

            def square(i, h, name, src, bias=0.0):
                act.wait_ge(S[src[0]][h], done(i))
                nc.scalar.activation(unit[name][h][:, :], src[1], ACT.Square, bias=bias).then_inc(S[name][h], 1)

            def root(i, h, name, produced, src):
                act.wait_ge(S[produced][h], done(i))
                nc.scalar.activation(unit[name][h][:, :], src, ACT.Sqrt, bias=v_eps).then_inc(S[name][h], 1)

            with act.Fori(0, PAIRS) as i:
                for h in range(2):
                    act.wait_ge(S["x_in"][h], 16 * done(i))
                    act.wait_ge(S["sums"][h], last(i))
                    nc.scalar.activation(xsq[h][:, :, :], xin[h][:, :, :], ACT.Square).then_inc(S["xsq"][h], 1)
                for h in range(2):
                    square(i, h, "musq", ("stat_mm", bank(h, 1)))
                for h in range(2):
                    root(i, h, "sd1", "var1", unit["var1"][h][:, :])
                for h in range(2):
                    square(i, h, "sq2", ("yc", unit["yc"][h][:, :]), c0c)
                for h in range(2):
                    root(i, h, "sd2", "var2_mm", bank(h, 1))
                for h in range(2):
                    square(i, h, "sq3", ("u_mm", bank(h, 0)), bp1c)
                for h in range(2):
                    root(i, h, "sd3", "var3_mm", bank(h, 1))
                for h in range(2):
                    act.wait_ge(S["t3"][h], done(i))
                    nc.scalar.activation(unit["act"][h][:, :], unit["t3"][h][:, :], ACT.Silu, bias=w("bep"),
                                         scale=w("gp")).then_inc(S["act"][h], 1)
                for h in range(2):
                    square(i, h, "sq4", ("h_mm", bank(h, 0)), bp2c)
                    act.wait_ge(S["h_out"][h], 16 * last(i))
                    nc.scalar.activation(unit["hs"][h][:, :], bank(h, 2), ACT.Identity, bias=w("bp2"))\
                        .then_inc(S["hs"][h], 1)
                for h in range(2):
                    root(i, h, "sd4", "var4_mm", bank(h, 1))

        @block.vector
        def _(dve):
            nc.vector.memset(zero[:, :], 0.0).then_inc(zeroed, 1)
            nc.vector.memset(v_eps, EPS)
            dve.wait_ge(wload, 16)
            dve.wait_ge(su_pe, 2)
            for c in range(2):
                nc.vector.tensor_scalar(w1g[:, c, :], ps[0:KF, c, 0:D], w3("ln1g", 2)[:, c, :], None, ALU.mult)\
                    .then_inc(su_dve, 1)
            dve.wait_ge(su_pe, 6)
            nc.vector.tensor_tensor(v_c0, ps[:, 4, 0:1], w("b1"), ALU.add).then_inc(su_dve, 1)
            nc.vector.tensor_tensor(v_bp1, ps[:, 5, 0:1], w("bp1"), ALU.add).then_inc(su_dve, 1)
            nc.vector.tensor_scalar(wp1g[:, :], ps[:, 2, 0:128], w("g2"), None, ALU.mult).then_inc(su_dve, 1)
            nc.vector.tensor_copy(wp2c[:, :], ps[:, 3, 0:128])
            nc.vector.tensor_tensor(wconv[:, :, :].rearrange("p a b -> p (a b)"), w("inx"), w("convw"), ALU.mult)
            nc.vector.tensor_copy(selbc[:, :, :].rearrange("p a b -> p (a b)"), w("selbc"))
            nc.vector.tensor_copy(selcb[:, :, :].rearrange("p a b -> p (a b)"), w("selcb"))
            dve.wait_ge(su_act, 1)
            nc.vector.tensor_scalar(aneg[:, :], aneg[:, :], -1.0, None, ALU.mult)
            dve.wait_ge(su_pe, 7)
            for c in range(2):
                nc.vector.tensor_tensor(w1c[:, c, :], w1g[:, c, :], ps[0:KF, 6, 0:D], ALU.subtract)
            dve.wait_ge(su_pe, 10)
            nc.vector.tensor_copy(c0c, ps[:, 7, 0:1])
            nc.vector.tensor_copy(bp1c, ps[:, 4, 0:1])
            nc.vector.tensor_copy(bp2c, ps[:, 5, 0:1])
            nc.vector.drain().then_inc(w_ready, 1)

            def recip(i, h, name, sd):
                dve.wait_ge(S[sd][h], done(i))
                nc.vector.reciprocal(unit[name][h][:, :], unit[sd][h][:, :]).then_inc(S[name][h], 1)

            def scaled(i, h, name, produced, src, bias, rs, dst=None):
                dve.wait_ge(S[rs][h], done(i))
                dve.wait_ge(S[produced][h], done(i))
                nc.vector.scalar_tensor_tensor(out=dst if dst is not None else unit[name][h][:, :], in0=src, scalar=bias, in1=unit[rs][h][:, :],
                                               op0=ALU.add, op1=ALU.mult).then_inc(S[name][h], 1)

            with dve.Fori(0, PAIRS) as i:
                for h in range(2):
                    dve.wait_ge(S["x_in"][h], 16 * done(i))
                    dve.wait_ge(S["xsq"][h], done(i))
                    dve.wait_ge(S["stat_mm"][h], last(i))
                    nc.vector.tensor_tensor(xsum[h][:, :], xin[h][:, 0, :], xin[h][:, 1, :], ALU.add)
                    nc.vector.tensor_tensor(qsum[h][:, :], xsq[h][:, 0, :], xsq[h][:, 1, :], ALU.add)\
                        .then_inc(S["sums"][h], 1)
                for h in range(2):
                    dve.wait_ge(S["musq"][h], done(i))
                    nc.vector.tensor_tensor(unit["var1"][h][:, :], bank(h, 2), unit["musq"][h][:, :], ALU.subtract)\
                        .then_inc(S["var1"][h], 1)
                for h in range(2):
                    recip(i, h, "rs1", "sd1")
                for h in range(2):
                    dve.wait_ge(S["rs1"][h], done(i))
                    dve.wait_ge(S["a_mm"][h], done(i))
                    nc.vector.tensor_tensor(unit["yc"][h][:, :], bank(h, 0), unit["rs1"][h][:, :], ALU.mult)\
                        .then_inc(S["yc"][h], 1)
                for h in range(2):
                    recip(i, h, "rs2", "sd2")
                for h in range(2):
                    scaled(i, h, "tok", "yc", unit["yc"][h][:, :], c0c, "rs2")
                for h in range(2):
                    recip(i, h, "rs3", "sd3")
                for h in range(2):
                    scaled(i, h, "t3", "u_mm", bank(h, 0), bp1c, "rs3")
                for h in range(2):
                    recip(i, h, "rs4", "sd4")
                for h in range(2):
                    dve.wait_ge(S["hn_out"][0], 16 * last(i))
                    scaled(i, h, "hns", "h_mm", bank(h, 0), bp2c, "rs4", hns[:, HT * h + 1:HT * h + 1 + HT])
                for h in range(2):
                    dve.wait_ge(S["hns"][h], done(i))
                nc.vector.tensor_copy(hns[:, 0:1], hns[:, NT:NT + 1])
                nc.vector.tensor_copy(hns[:, NT + 1:NT + 2], hns[:, 1:2]).then_inc(S["ends"][0], 1)


def mamba(nc, ps, sem, w, w3, h_d, hn_d, h2_d, wconv, aneg, selbc):
    with ExitStack() as ctx:
        def sb(name, shape, dt=F32):
            return ctx.enter_context(nc.sbuf_tensor(name, shape, dt))

        hf = sb("hf", [128, TP])
        hb = sb("hb", [128, TP])
        hres = sb("hres", [128, NT])
        xc = [sb(f"xc{k}", [128, TP]) for k in range(2)]
        gate = [sb(f"gate{k}", [128, TP]) for k in range(2)]
        bcs = [sb(f"bcs{k}", [128, 2, 2, TP]) for k in range(2)]
        dtr = sb("dtr", [32, TP])
        parts = [sb(f"parts{k}", [128, 3, TP]) for k in range(3)]
        stack = sb("stack", [96, NQ, 3, TP])
        da, dbx, hs, ch, pc, cp = ([sb(f"{n}{k}", [128, TP]) for k in range(2)]
                                   for n in ("da", "dbx", "hst", "chs", "pcum", "cps"))
        delta = sb("delta", [128, 2, 2])
        wdel = sb("wdel", [128, QJ, 2, 32])
        yall = sb("yall", [128, 3, TP])
        fin = sb("fin", [128, L + 1])
        osb = [sb(f"osb{k}", [128, HT]) for k in range(2)]
        ones = sb("ones", [128, 1])

        per_tile = ("dt_bc", "u_bc", "s_bc", "da_done", "p_done", "dbx_done", "scan_done", "ch_done", "del_done",
                    "del2_done", "wdel_done", "cp_done", "y_mm", "w_mm")
        per_image = dict(conv_mm=2, xc_done=2, z_mm=2, g_done=2, dtr_mm=2, dtr_done=2, dt_mm=2, pre_done=2, abs_done=1, relu_done=1, e_done=1, ln_done=1, r_done=1, sum_done=1, c_done=1, dt_done=1, bc_mm=8,
                         bc_done=8, s_done=1, u_done=1, r1_done=1, r2_done=1, yd_done=1, e0_done=1, wg_done=2,
                         f_done=2, out_mm=6, out_done=6, evac=12, hres_in=16, stk=16 * 3 * NQ)
        T = {n: sem("m_" + n) for n in per_tile}
        S = {n: sem("m_" + n) for n in per_image if n != "stk"}
        stk = [sem(f"m_stk{q}") for q in range(NQ)]
        q_used = [sem(f"m_q_used{q}") for q in range(NQ)]
        hfb_in, stored, ready = sem("hfb_in"), [sem(f"h2_stored{k}") for k in range(2)], sem("m_ready")
        READY = 2

        def tile(n, t):
            return n * TILES + (t + 3)

        def img(name, n, c):
            k = per_image[name]
            return n * k + (k + c)

        BX, BU, BY, BG = 0, 2, 4, 6

        def halves(bank):
            return ps[:, bank:bank + 2, 0:TH]

        def two(ap):
            return ap.rearrange("p (a b) -> p a b", a=2)

        def hi(ap):
            return ap.bitcast(BF16)[..., 1::2]

        block = ctx.enter_context(nc.Block())

        @block.sync
        def _(sp):
            def load_hn(pair, im):
                rows = slice(64 * im, 64 * im + 64)
                sp.dma_start(hf[0:64, 0:TC], hn_d[pair, rows, 1:TP]).then_inc(hfb_in, 16)
                sp.dma_start(hf[64:128, 1:TC], hn_d[pair, rows, 1:TC]).then_inc(hfb_in, 16)
                sp.dma_start(hb[0:64, 0:TC], hn_d[pair, rows, 0:TC]).then_inc(hfb_in, 16)
                sp.dma_start(hb[64:128, 0:NT], hn_d[pair, rows, 1:TC]).then_inc(hfb_in, 16)

            def restack(m, quarters):
                nth = img("r2_done", m, 1)
                if type(m) is not int:
                    nth = sp.snap(nth)
                if 0 in quarters:
                    sp.wait_ge(S["r2_done"], nth)
                for q in quarters:
                    if type(m) is not int:
                        sp.wait_ge(q_used[q], nth)
                    for k in range(3):
                        sp.dma_start(stack[32 * k:32 * k + 32, q, :, :], parts[k][32 * q:32 * q + 32, :, :])\
                            .then_inc(stk[q], 16)

            sp.wait_ge(ready, READY)
            load_hn(0, 0)
            restack(0, range(NQ))

            with sp.Fori(0, PAIRS) as i:
                following = sp.snap(i + 1)
                for par in range(2):
                    n = i * 2 + par
                    sp.wait_ge(S["z_mm"], img("z_mm", n, 2))
                    load_hn(i if par == 0 else following, 1 - par)
                    im = slice(64 * (1 - par), 64 * (1 - par) + 64)
                    sp.wait_ge(S["out_done"], img("out_done", n, 0))
                    sp.dma_start(hres[im, :], h_d[i + par, im, :]).then_inc(S["hres_in"], 16)
                    restack(n + 1, range(NQ - 1))
                    for c in range(6):
                        sp.wait_ge(S["out_done"], img("out_done", n, c + 1))
                        sp.dma_start(h2_d[i + par, im, HT * c:HT * c + HT], osb[c % 2][im, :])\
                            .then_inc(stored[c % 2], 16)
                    restack(n + 1, (NQ - 1,))
            im = slice(64, 128)
            sp.wait_ge(S["out_done"], img("out_done", B, 0))
            sp.dma_start(hres[im, :], h_d[PAIRS, im, :]).then_inc(S["hres_in"], 16)
            for c in range(6):
                sp.wait_ge(S["out_done"], img("out_done", B, c + 1))
                sp.dma_start(h2_d[PAIRS, im, HT * c:HT * c + HT], osb[c % 2][im, :]).then_inc(stored[c % 2], 16)
            for k in range(2):
                sp.wait_ge(stored[k], 16 + 16 * 3 * (B + 1))

        @block.gpsimd
        def _(pool):
            for n in per_tile:
                pool.sem_inc(T[n], 2)
            for n, k in per_image.items():
                if n != "stk":
                    pool.sem_inc(S[n], k)
            for q in range(NQ):
                pool.sem_inc(stk[q], 48)
                pool.sem_inc(q_used[q], 2)
            for k in range(2):
                pool.sem_inc(stored[k], 16)
            pool.sem_inc(hfb_in, 64)
            nc.gpsimd.memset(wdel[:, :, :, :], 0.0)
            nc.gpsimd.memset(yall[:, :, :], 0.0)
            for k in range(2):
                nc.gpsimd.memset(gate[k][:, :], 0.0)
            nc.gpsimd.drain().then_inc(ready, 1)
            pool.wait_ge(ready, READY)

            def prepare_u(m, k):
                pool.wait_ge(S["dt_done"], img("dt_done", m, 1))
                pool.wait_ge(S["xc_done"], img("xc_done", m, 2))
                nc.gpsimd.tensor_tensor(parts[0][:, 2, 0:TC], parts[0][:, 0, 0:TC], xc[k][:, 0:TC], ALU.mult)\
                    .then_inc(S["u_done"], 1)

            def split(m, k):
                if k == 0:
                    pool.wait_ge(S["s_done"], img("s_done", m, 1))
                    pool.wait_ge(S["u_done"], img("u_done", m, 1))
                else:
                    pool.wait_ge(S["r1_done"], img("r1_done", m, 1))
                name = ("r1_done", "r2_done")[k]
                for v in range(3):
                    op = nc.gpsimd.tensor_tensor(parts[k + 1][:, v, 0:TC], parts[k][:, v, 0:TC],
                                                 hi(parts[k][:, v, 0:TC]), ALU.subtract)
                op.then_inc(S[name], 1)

            def finish(n, k, step):
                g = gate[k]
                if step == 0:
                    pool.wait_ge(S["yd_done"], img("yd_done", n, 1))
                    pool.wait_ge(S["out_mm"], img("out_mm", n, 0))
                    nc.gpsimd.tensor_tensor(fin[:, 0:TC], yall[:, 0, 0:TC], g[:, 0:TC], ALU.mult)\
                        .then_inc(S["e0_done"], 1)
                else:
                    at = TC + NT * (step - 1)
                    nc.gpsimd.tensor_tensor(yall[:, step, 1:TC], yall[:, step, 1:TC], g[:, 1:TC], ALU.mult)\
                        .then_inc(S["wg_done"], 1)
                    pool.wait_ge(S["e0_done"], img("e0_done", n, 1))
                    pool.wait_ge(S["wg_done"], img("wg_done", n, step))
                    nc.gpsimd.tensor_tensor(fin[:, at:at + NT], yall[:, step, 1:TC], fin[:, 1:TC], ALU.add)\
                        .then_inc(S["f_done"], 1)

            prepare_u(0, 0)
            split(0, 0)
            split(0, 1)
            with pool.Fori(0, PAIRS) as i:
                for par in range(2):
                    n = i * 2 + par
                    for t in range(TILES):
                        k, d = t % 2, t // NJ
                        pool.wait_ge(T["p_done"], tile(n, t))
                        pool.wait_ge(T["w_mm"], tile(n, t - 2))
                        nc.gpsimd.tensor_tensor(cp[k][:, 0:TC], pc[k][:, 0:TC], bcs[par][:, d, 1, 0:TC], ALU.mult)\
                            .then_inc(T["cp_done"], 1)
                        if t < 3:
                            finish(n, 1 - par, t)
                        if t == 8:
                            prepare_u(n + 1, 1 - par)
                        if t in (9, 11):
                            split(n + 1, (t - 9) // 2)
            for step in range(3):
                finish(B, 1, step)

        @block.tensor
        def _(pe):
            def bc(bank, q, j, v, name):
                for a in range(2):
                    mm = nc.tensor.matmul(ps[:, bank + a, 0:TH], selbc[:, j, :],
                                          hi(stack[:, q, v, :])[:, TH * a:TH * a + TH], start=True, stop=True)
                mm.then_inc(T[name], 1)

            def ahead(n, t):
                q, j = t // QJ, t % QJ
                if j == 0:
                    pe.wait_ge(stk[q], n * 48 + 96)
                pe.wait_ge(T["p_done"], tile(n, t - 1))
                bc(BX, q, j, 0, "dt_bc")
                pe.wait_ge(T["dbx_done"], tile(n, t - 1))
                bc(BU, q, j, 2, "u_bc")

            def ahead_s(n, t):
                pe.wait_ge(T["da_done"], tile(n, t))
                bc(BX, t // QJ, t % QJ, 1, "s_bc")

            def rows_of(d, f, size):
                return hf[:, f:f + size] if d == 0 else hb[:, NT - f::-1][:, 0:size]

            def conv(m):
                pe.wait_ge(hfb_in, m * 64 + 128)
                pe.wait_ge(S["out_done"], img("out_done", m, -6 if type(m) is not int else 0))
                pe.wait_ge(S["bc_done"], img("bc_done", m, 0))
                for a in range(2):
                    for d in range(2):
                        mm = nc.tensor.matmul(ps[64 * d:64 * d + 64, BG + a, 0:TH - a], wconv[:, d, :],
                                              rows_of(d, TH * a, TH - a), start=True, stop=True)
                    mm.then_inc(S["conv_mm"], 1)

            def gates(m):
                for a in range(2):
                    pe.wait_ge(S["xc_done"], img("xc_done", m, a + 1))
                    for d in range(2):
                        mm = nc.tensor.matmul(ps[64 * d:64 * d + 64, BG + a, 0:TH - a], w3("inz", 2)[:, d, :],
                                              rows_of(d, TH * a, TH - a), start=True, stop=True)
                    mm.then_inc(S["z_mm"], 1)

            def dt_low(m, k):
                for a in range(2):
                    pe.wait_ge(S["g_done"], img("g_done", m, a + 1))
                    nc.tensor.matmul(ps[0:32, BG + a, 0:TH], w("wdtr"), xc[k][:, TH * a:TH * a + TH],
                                     start=True, stop=True).then_inc(S["dtr_mm"], 1)

            def dt_full(m):
                for a in range(2):
                    pe.wait_ge(S["dtr_done"], img("dtr_done", m, a + 1))
                    nc.tensor.matmul(ps[:, BG + a, 0:TH], w("wdt"), dtr[:, TH * a:TH * a + TH],
                                     start=True, stop=True).then_inc(S["dt_mm"], 1)

            def b_or_c(m, k, step):
                d, which = step // 2, step % 2
                for a in range(2):
                    if step == 0:
                        pe.wait_ge(S["pre_done"], img("pre_done", m, a + 1))
                    else:
                        pe.wait_ge(S["bc_done"], img("bc_done", m, 2 * step - 1 + a))
                    nc.tensor.matmul(ps[:, BG + a, 0:TH], w3("wbc", 2)[64 * d:64 * d + 64, which, :],
                                     xc[k][64 * d:64 * d + 64, TH * a:TH * a + TH], start=True, stop=True)\
                        .then_inc(S["bc_mm"], 1)

            def project(n, im, c, before):
                wout = w3("wout", 2)
                if c == 0:
                    pe.wait_ge(S["f_done"], img("f_done", n, 2))
                if c < 2:
                    pe.wait_ge(S["bc_done"], before + c)
                else:
                    pe.wait_ge(S["out_done"], img("out_done", n, c - 1))
                lo = HT * c
                rev = fin[:, L - 1 - lo:L - 1 - lo - HT:-1] if L - 1 - lo - HT >= 0 else fin[:, L - 1 - lo::-1]
                o = ps[64 * im:64 * im + 64, BG + c % 2, 0:HT]
                nc.tensor.matmul(o, wout[:, 0, :], fin[:, lo:lo + HT], start=True, stop=False)
                nc.tensor.matmul(o, wout[:, 1, :], rev, start=False, stop=True).then_inc(S["out_mm"], 1)

            pe.wait_ge(ready, READY)
            conv(0)
            gates(0)
            dt_low(0, 0)
            dt_full(0)
            for step in range(4):
                b_or_c(0, 0, step)
            ahead(0, 0)
            ahead_s(0, 0)
            with pe.Fori(0, PAIRS) as i:
                for par in range(2):
                    n = i * 2 + par
                    for t in range(TILES):
                        nn, tt = (n, t + 1) if t + 1 < TILES else (n + 1, 0)
                        ahead(nn, tt)
                        if t == 3:
                            conv(n + 1)
                        if t == 4:
                            gates(n + 1)
                        if t == 5:
                            dt_low(n + 1, 1 - par)
                        if t == 6:
                            dt_full(n + 1)
                        if 7 <= t < 11:
                            b_or_c(n + 1, 1 - par, t - 7)
                        if 11 <= t < 14:
                            for c in (2 * (t - 11), 2 * (t - 11) + 1):
                                project(n, 1 - par, c, img("bc_done", n + 1, 7))
                        ahead_s(nn, tt)
                        k, j = t % 2, t % QJ
                        pe.wait_ge(T["ch_done"], tile(n, t))
                        if j == 0:
                            pe.wait_ge(S["evac"], img("evac", n, 3 * (t // QJ)))
                        for a in range(2):
                            mm = nc.tensor.matmul(ps[0:32, BY + a, 0:TH - a], w3("ysel", QJ)[:, j, :],
                                                  ch[k][:, TH * a:TH * a + TH - a], start=(j == 0), stop=(j == QJ - 1))
                            if a == 0 and j == QJ - 2:
                                mm.then_inc(q_used[t // QJ], 1)
                        mm.then_inc(T["y_mm"], 1)
                        pe.wait_ge(T["cp_done"], tile(n, t))
                        pe.wait_ge(T["wdel_done"], tile(n, t))
                        for a in range(2):
                            mm = nc.tensor.matmul(ps[64:128, BY + a, 0:TH - a],
                                                  wdel[:, j, :, :].rearrange("p a b -> p (a b)"),
                                                  cp[k][:, TH * a:TH * a + TH - a], start=(j == 0), stop=(j == QJ - 1))
                        mm.then_inc(T["w_mm"], 1)
            for c in range(6):
                project(B, 1, c, img("bc_done", B, 7))

        @block.scalar
        def _(act):
            def decay(n, t):
                k = t % 2
                act.wait_ge(T["dt_bc"], tile(n, t))
                act.wait_ge(T["scan_done"], tile(n, t - 2))
                nc.scalar.activation(two(da[k][:, :]), halves(BX), ACT.Exp, scale=aneg[:, t:t + 1])\
                    .then_inc(T["da_done"], 1)
                act.wait_ge(T["s_bc"], tile(n, t))
                act.wait_ge(T["cp_done"], tile(n, t - 2))
                act.wait_ge(T["del2_done"], tile(n, t - 2))
                nc.scalar.activation(two(pc[k][:, :]), halves(BX), ACT.Exp, scale=aneg[:, t:t + 1])\
                    .then_inc(T["p_done"], 1)

            def convolved(m, k):
                if type(m) is not int:
                    act.wait_ge(S["yd_done"], img("yd_done", m, 0))
                act.wait_ge(S["bc_mm"], img("bc_mm", m, 0))
                act.wait_ge(S["u_done"], img("u_done", m, 0))
                for a in range(2):
                    act.wait_ge(S["conv_mm"], img("conv_mm", m, a + 1))
                    nc.scalar.activation(xc[k][:, TH * a:TH * a + TH - a], ps[:, BG + a, 0:TH - a], ACT.Silu,
                                         bias=w("convb")).then_inc(S["xc_done"], 1)

            def gated(m, k):
                if type(m) is not int:
                    act.wait_ge(S["wg_done"], img("wg_done", m, 0))
                    act.wait_ge(S["e0_done"], img("e0_done", m, 0))
                for a in range(2):
                    act.wait_ge(S["z_mm"], img("z_mm", m, a + 1))
                    nc.scalar.activation(gate[k][:, TH * a:TH * a + TH - a], ps[:, BG + a, 0:TH - a], ACT.Silu)\
                        .then_inc(S["g_done"], 1)

            def low(m):
                act.wait_ge(S["dt_mm"], img("dt_mm", m, 0))
                for a in range(2):
                    act.wait_ge(S["dtr_mm"], img("dtr_mm", m, a + 1))
                    nc.scalar.activation(dtr[:, TH * a:TH * a + TH], ps[0:32, BG + a, 0:TH], ACT.Copy)\
                        .then_inc(S["dtr_done"], 1)

            def soft(m):
                for q in range(NQ):
                    act.wait_ge(stk[q], m * 48 + 48)
                for a in range(2):
                    act.wait_ge(S["dt_mm"], img("dt_mm", m, a + 1))
                    nc.scalar.activation(parts[0][:, 0, TH * a:TH * a + TH - a], ps[:, BG + a, 0:TH - a], ACT.Identity,
                                         bias=w("dtb")).then_inc(S["pre_done"], 1)
                act.wait_ge(S["pre_done"], img("pre_done", m, 2))
                nc.scalar.activation(parts[1][:, 0, 0:TC], parts[0][:, 0, 0:TC], ACT.Abs).then_inc(S["abs_done"], 1)
                act.wait_ge(S["abs_done"], img("abs_done", m, 1))
                nc.scalar.activation(parts[1][:, 0, 0:TC], parts[1][:, 0, 0:TC], ACT.Exp, scale=-1.0)\
                    .then_inc(S["e_done"], 1)
                act.wait_ge(S["e_done"], img("e_done", m, 1))
                nc.scalar.activation(parts[2][:, 0, 0:TC], parts[1][:, 0, 0:TC], ACT.Ln, bias=ones[:, :])\
                    .then_inc(S["ln_done"], 1)

            def b_or_c(m, k, step):
                for a in range(2):
                    act.wait_ge(S["bc_mm"], img("bc_mm", m, 2 * step + a + 1))
                    nc.scalar.activation(bcs[k][:, step // 2, step % 2, TH * a:TH * a + TH], ps[:, BG + a, 0:TH],
                                         ACT.Copy).then_inc(S["bc_done"], 1)

            def evacuate(n, q):
                act.wait_ge(S["f_done"], img("f_done", n, 2))
                act.wait_ge(T["y_mm"], tile(n, QJ * q + QJ - 1))
                act.wait_ge(T["w_mm"], tile(n, QJ * q + QJ - 1))
                for k, rows in ((0, slice(0, 32)), (1, slice(64, 96)), (2, slice(96, 128))):
                    for a in range(2):
                        op = nc.scalar.activation(yall[32 * q:32 * q + 32, k, TH * a:TH * a + TH - a],
                                                  ps[rows, BY + a, 0:TH - a], ACT.Copy)
                    op.then_inc(S["evac"], 1)

            act.wait_ge(ready, READY)
            convolved(0, 0)
            gated(0, 0)
            low(0)
            soft(0)
            for step in range(4):
                b_or_c(0, 0, step)
            decay(0, 0)
            with act.Fori(0, PAIRS) as i:
                for par in range(2):
                    n = i * 2 + par
                    for t in range(TILES):
                        if t + 1 < TILES:
                            decay(n, t + 1)
                        else:
                            decay(n + 1, 0)
                        if t == 3:
                            convolved(n + 1, 1 - par)
                        if t == 4:
                            gated(n + 1, 1 - par)
                        if t == 5:
                            low(n + 1)
                        if t == 6:
                            soft(n + 1)
                        if 7 <= t < 11:
                            b_or_c(n + 1, 1 - par, t - 7)
                        if t % QJ == QJ - 1:
                            evacuate(n, t // QJ)

        @block.vector
        def _(dve):
            nc.vector.memset(ones[:, :], 1.0)
            nc.vector.memset(hf[64:128, 0:1], 0.0)
            nc.vector.memset(hb[64:128, NT:TC], 0.0)
            for k in range(2):
                nc.vector.memset(xc[k][:, :], 0.0)
            for k in range(3):
                nc.vector.memset(parts[k][:, :, TC:TP], 0.0)
            nc.vector.memset(parts[0][:, 1, 0:1], 0.0)
            nc.vector.drain().then_inc(ready, 1)
            dve.wait_ge(ready, READY)

            def softplus(m):
                dve.wait_ge(S["abs_done"], img("abs_done", m, 1))
                nc.vector.tensor_scalar(parts[0][:, 0, 0:TC], parts[0][:, 0, 0:TC], 0.0, None, ALU.max)\
                    .then_inc(S["relu_done"], 1)
                e, lost = parts[1][:, 0, 0:TC], parts[1][:, 1, 0:TC]
                total = parts[2][:, 0, 0:TC]
                dve.wait_ge(S["e_done"], img("e_done", m, 1))
                nc.vector.tensor_scalar(lost, e, 1.0, -1.0, ALU.add, ALU.add).then_inc(S["r_done"], 1)
                dve.wait_ge(S["ln_done"], img("ln_done", m, 1))
                dve.wait_ge(S["relu_done"], img("relu_done", m, 1))
                nc.vector.tensor_tensor(total, total, parts[0][:, 0, 0:TC], ALU.add).then_inc(S["sum_done"], 1)
                dve.wait_ge(S["r_done"], img("r_done", m, 1))
                nc.vector.tensor_tensor(lost, e, lost, ALU.subtract).then_inc(S["c_done"], 1)
                dve.wait_ge(S["c_done"], img("c_done", m, 1))
                dve.wait_ge(S["sum_done"], img("sum_done", m, 1))
                nc.vector.tensor_tensor(parts[0][:, 0, 0:TC], total, lost, ALU.add).then_inc(S["dt_done"], 1)

            def cumsum(m):
                dve.wait_ge(S["dt_done"], img("dt_done", m, 1))
                nc.vector.tensor_tensor_scan(parts[0][:, 1, 1:TC], ones[:, :].to_broadcast([128, NT]),
                                             parts[0][:, 0, 1:TC], 0.0, ALU.mult, ALU.add).then_inc(S["s_done"], 1)

            def skip_add(n, k):
                dve.wait_ge(S["evac"], img("evac", n, 0))
                nc.vector.scalar_tensor_tensor(out=yall[:, 0, 0:TC], in0=xc[k][:, 0:TC], scalar=w("dvec"),
                                               in1=yall[:, 0, 0:TC], op0=ALU.mult, op1=ALU.add)\
                    .then_inc(S["yd_done"], 1)

            def add_residual(n, im, c):
                rows = slice(64 * im, 64 * im + 64)
                if c == 0:
                    dve.wait_ge(S["hres_in"], img("hres_in", n, 16))
                dve.wait_ge(S["out_mm"], img("out_mm", n, c + 1))
                dve.wait_ge(stored[c % 2], n * 48 + (16 + 16 * (c // 2)))
                nc.vector.tensor_tensor(osb[c % 2][rows, :], ps[rows, BG + c % 2, 0:HT],
                                        hres[rows, HT * (c % 2):HT * (c % 2) + HT], ALU.add)\
                    .then_inc(S["out_done"], 1)

            softplus(0)
            cumsum(0)
            with dve.Fori(0, PAIRS) as i:
                for par in range(2):
                    n = i * 2 + par
                    for t in range(TILES):
                        k, d, j = t % 2, t // NJ, t % QJ
                        if t in (0, NJ):
                            dve.wait_ge(S["bc_done"], img("bc_done", n, 4 + 4 * d))
                        dve.wait_ge(T["u_bc"], tile(n, t))
                        dve.wait_ge(T["scan_done"], tile(n, t - 2))
                        nc.vector.tensor_tensor(two(dbx[k][:, :]), halves(BU), two(bcs[par][:, d, 0, :]), ALU.mult)\
                            .then_inc(T["dbx_done"], 1)
                        dve.wait_ge(T["da_done"], tile(n, t))
                        dve.wait_ge(T["dbx_done"], tile(n, t))
                        dve.wait_ge(T["ch_done"], tile(n, t - 2))
                        nc.vector.tensor_tensor_scan(hs[k][:, 0:TC], da[k][:, 0:TC], dbx[k][:, 0:TC], 0.0,
                                                     ALU.mult, ALU.add).then_inc(T["scan_done"], 1)
                        dve.wait_ge(T["scan_done"], tile(n, t))
                        dve.wait_ge(T["y_mm"], tile(n, t - 2))
                        nc.vector.tensor_tensor(ch[k][:, 0:TC], hs[k][:, 0:TC], bcs[par][:, d, 1, 0:TC], ALU.mult)\
                            .then_inc(T["ch_done"], 1)
                        dve.wait_ge(T["p_done"], tile(n, t))
                        dve.wait_ge(T["wdel_done"], tile(n, t - 2))
                        nc.vector.tensor_tensor(delta[:, k, 0:1], hs[k][:, NT:TC], hs[k][:, 0:1], ALU.subtract)\
                            .then_inc(T["del_done"], 1)
                        dve.wait_ge(T["del_done"], tile(n, t))
                        nc.vector.scalar_tensor_tensor(out=delta[:, k, 1:2], in0=pc[k][:, NT:TC],
                                                       scalar=delta[:, k, 0:1], in1=delta[:, k, 0:1],
                                                       op0=ALU.mult, op1=ALU.add).then_inc(T["del2_done"], 1)
                        dve.wait_ge(T["w_mm"], tile(n, t - 2))
                        dve.wait_ge(T["del2_done"], tile(n, t))
                        for c in range(2):
                            op = nc.vector.tensor_scalar(wdel[:, j, c, DB * j:DB * j + DB], w("mask8"),
                                                         delta[:, k, c:c + 1], None, ALU.mult)
                        op.then_inc(T["wdel_done"], 1)
                        if t == 0:
                            skip_add(n, 1 - par)
                        if t == 6:
                            softplus(n + 1)
                        if t == 8:
                            cumsum(n + 1)
                        if 12 <= t < 15:
                            for c in (2 * (t - 12), 2 * (t - 12) + 1):
                                add_residual(n, 1 - par, c)
            skip_add(B, 1)
            for c in range(6):
                add_residual(B, 1, c)


def experts(nc, ps, sem, w, w3, h2_d, out, selcb, v_eps):
    UNITS = PAIRS * NCK
    G = NTT * 2
    with ExitStack() as ctx:
        def sb(name, shape, dt=F32):
            return ctx.enter_context(nc.sbuf_tensor(name, shape, dt))

        hx, xn, res, osb = ([sb(f"{n}{k}", [128, CK]) for k in range(2)] for n in ("hx", "xn", "res", "oute"))
        cparts = [sb(f"cparts{k}", [80, CK]) for k in range(2)]
        sq, sd, rs = sb("sqe", [128, CK]), sb("sde", [128, CK]), sb("rse", [128, CK])
        small = {n: sb("r_" + n, [TT, G, NE]) for n in
                 ("shift", "e", "p", "eq1", "key1", "sel1", "rest", "eq2", "key2", "sel2", "both", "comb")}
        one = {n: sb("r1_" + n, [TT, G]) for n in ("mx", "sum", "rsum", "m1", "k1", "m2", "k2", "den", "rden")}
        hid, scaled = ([sb(f"{n}{k}", [128, CK]) for k in range(2)] for n in ("hid", "hsc"))

        per_unit = dict(c_mm=1, sq=1, v_mm=1, sd=1, rs=1, xn=1, res=1, lg_mm=1, shift=1, e=1, route=21,
                        tr_mm=1, cb_hi=1, cb_mid=1, cb_lo=1, b_mm=8, h_mm=8, hid=8, scaled=8, l2_mm=8, o_done=1)
        S = {n: sem("e_" + n) for n in per_unit}
        hx_in = [sem(f"hx_in{k}") for k in range(2)]
        o_out = [sem(f"o_out{k}") for k in range(2)]
        ready = sem("e_ready")

        def unit(name, n, c):
            k = per_unit[name]
            return n * k + (2 * k + c)

        BC_, BV, BL, BB, BH, BO = 0, 1, 2, 3, 5, 7

        def hi(ap):
            return ap.bitcast(BF16)[..., 1::2]

        def wide(ap):
            return ap.unsqueeze(2).to_broadcast([TT, G, NE])

        block = ctx.enter_context(nc.Block())

        @block.sync
        def _(sp):
            def load(p, c, m, k):
                sp.wait_ge(S["res"], unit("res", m - 1, 0))
                sp.wait_ge(S["c_mm"], unit("c_mm", m - 1, 0))
                sp.dma_start(hx[k][:, :], h2_d[p + 1, :, bass.ds(c * CK, CK)] if type(c) is not int
                             else h2_d[p + 1, :, CK * c:CK * c + CK]).then_inc(hx_in[k], 16)

            sp.wait_ge(ready, 1)
            load(0, 0, 0, 0)
            load(0, 1, 1, 1)
            with sp.Fori(0, PAIRS) as p:
                for c in range(NCK):
                    n = p * NCK + c
                    if c + 2 < NCK:
                        load(p, c + 2, n + 2, c % 2)
                    else:
                        load(p + 1, c + 2 - NCK, n + 2, c % 2)
                    sp.wait_ge(S["o_done"], unit("o_done", n, 1))
                    sp.dma_start(out[p, :, CK * c:CK * c + CK], osb[c % 2][:, :]).then_inc(o_out[c % 2], 16)
            for k in range(2):
                sp.wait_ge(hx_in[k], 16 * (UNITS // 2 + 1))
                sp.wait_ge(o_out[k], 16 * (UNITS // 2 + 1))

        @block.gpsimd
        def _(pool):
            for n, k in per_unit.items():
                pool.sem_inc(S[n], 2 * k)
            for k in range(2):
                pool.sem_inc(o_out[k], 16)
            for k in range(2):
                nc.gpsimd.memset(cparts[k][:, :], 0.0)
            nc.gpsimd.drain().then_inc(ready, 1)

            def residual(m, k, loads):
                pool.wait_ge(hx_in[k], 16 * loads)
                pool.wait_ge(S["xn"], unit("xn", m, 1))
                pool.wait_ge(S["o_done"], unit("o_done", m - 1, 0))
                nc.gpsimd.tensor_tensor(res[k][:, :], hx[k][:, :], xn[k][:, :], ALU.add).then_inc(S["res"], 1)

            residual(0, 0, 1)
            with pool.Fori(0, UNITS // 2) as i:
                for k in range(2):
                    residual(i * 2 + (k + 1), 1 - k, i + 1 + k)

        @block.tensor
        def _(pe):
            def centre(m, k, loads):
                pe.wait_ge(hx_in[k], 16 * loads)
                pe.wait_ge(S["xn"], unit("xn", m, 0))
                nc.tensor.matmul(ps[:, BC_, 0:CK], w("cen"), hx[k][:, :], start=True, stop=True).then_inc(S["c_mm"], 1)

            def variance(m):
                pe.wait_ge(S["cb_lo"], unit("cb_lo", m, 0))
                pe.wait_ge(S["sq"], unit("sq", m, 1))
                nc.tensor.matmul(ps[:, BV, 0:CK], w("avg"), sq[:, :], start=True, stop=True).then_inc(S["v_mm"], 1)

            def logits(m, k):
                pe.wait_ge(S["xn"], unit("xn", m, 1))
                pe.wait_ge(S["shift"], unit("shift", m, 0))
                for t in range(NTT):
                    mm = nc.tensor.matmul(ps[0:TT, BL, 2 * NE * t:2 * NE * t + 2 * NE], xn[k][:, TT * t:TT * t + TT],
                                          w("router"), start=True, stop=True)
                mm.then_inc(S["lg_mm"], 1)

            def turn(m):
                pe.wait_ge(S["route"], unit("route", m, 21))
                pe.wait_ge(S["sd"], unit("sd", m, 1))
                for t in range(NTT):
                    mm = nc.tensor.transpose(ps[0:2 * NE, BV, TT * t:TT * t + TT],
                                             small["comb"][:, 2 * t:2 * t + 2, :].rearrange("p a b -> p (a b)"),
                                             w("ident"))
                mm.then_inc(S["tr_mm"], 1)

            def first(n, k, e):
                im, q = e // 4, e % 4
                rows = slice(64 * im, 64 * im + 64)
                if e == 0:
                    pe.wait_ge(S["cb_lo"], unit("cb_lo", n, 1))
                pe.wait_ge(S["scaled"], unit("scaled", n, e - 1))
                nc.tensor.matmul(ps[:, BB + e % 2, 0:CK], selcb[:, e, :], hi(cparts[k][:, :]),
                                 start=True, stop=True).then_inc(S["b_mm"], 1)
                pe.wait_ge(S["hid"], unit("hid", n, e - 1))
                nc.tensor.matmul(ps[:, BH + e % 2, 0:CK], w3("ew1", 4)[rows, q, :], xn[k][rows, :],
                                 start=True, stop=True).then_inc(S["h_mm"], 1)

            def second(n, k, e):
                im, q = e // 4, e % 4
                o = ps[64 * im:64 * im + 64, BO, 0:CK]
                if q == 0:
                    if im == 0:
                        pe.wait_ge(S["o_done"], unit("o_done", n, 0))
                    nc.tensor.matmul(o, w3("eb2", 2)[:, im, :], cparts[k][0:2 * NE, :], start=True, stop=False)
                pe.wait_ge(S["scaled"], unit("scaled", n, e + 1))
                nc.tensor.matmul(o, w3("ew2", 4)[:, q, :], scaled[e % 2][:, :], start=False, stop=(q == 3))\
                    .then_inc(S["l2_mm"], 1)

            pe.wait_ge(ready, 1)
            centre(0, 0, 1)
            variance(0)
            logits(0, 0)
            turn(0)
            with pe.Fori(0, UNITS // 2) as i:
                for k in range(2):
                    n = i * 2 + k
                    for e in range(8):
                        first(n, k, e)
                        if e == 0:
                            centre(n + 1, 1 - k, i + 1 + k)
                        if e == 1:
                            variance(n + 1)
                        if e == 3:
                            logits(n + 1, 1 - k)
                        if e == 7:
                            turn(n + 1)
                        if e > 0:
                            second(n, k, e - 1)
                    second(n, k, 7)

        @block.scalar
        def _(act):
            def square(m):
                act.wait_ge(S["c_mm"], unit("c_mm", m, 1))
                act.wait_ge(S["v_mm"], unit("v_mm", m, 0))
                nc.scalar.activation(sq[:, :], ps[:, BC_, 0:CK], ACT.Square).then_inc(S["sq"], 1)

            def root(m):
                act.wait_ge(S["v_mm"], unit("v_mm", m, 1))
                act.wait_ge(S["rs"], unit("rs", m, 0))
                nc.scalar.activation(sd[:, :], ps[:, BV, 0:CK], ACT.Sqrt, bias=v_eps).then_inc(S["sd"], 1)

            def exponent(m):
                act.wait_ge(S["shift"], unit("shift", m, 1))
                act.wait_ge(S["route"], unit("route", m, 0))
                nc.scalar.activation(small["e"][:, :, :], small["shift"][:, :, :], ACT.Exp).then_inc(S["e"], 1)

            def gelu(n, e):
                act.wait_ge(S["h_mm"], unit("h_mm", n, e + 1))
                act.wait_ge(S["scaled"], unit("scaled", n, e - 1))
                nc.scalar.activation(hid[e % 2][:, :], ps[:, BH + e % 2, 0:CK], ACT.Gelu, bias=w("eb1")[:, e % 4:e % 4 + 1])\
                    .then_inc(S["hid"], 1)

            square(0)
            root(0)
            exponent(0)
            with act.Fori(0, UNITS // 2) as i:
                for k in range(2):
                    n = i * 2 + k
                    for e in range(8):
                        gelu(n, e)
                        if e == 0:
                            square(n + 1)
                        if e == 1:
                            root(n + 1)
                        if e == 4:
                            exponent(n + 1)

        @block.vector
        def _(dve):
            def normalize(m, k):
                dve.wait_ge(S["sd"], unit("sd", m, 1))
                nc.vector.reciprocal(rs[:, :], sd[:, :]).then_inc(S["rs"], 1)
                dve.wait_ge(S["rs"], unit("rs", m, 1))
                dve.wait_ge(S["h_mm"], unit("h_mm", m - 1, 0))
                dve.wait_ge(S["res"], unit("res", m - 1, 0))
                nc.vector.tensor_tensor(xn[k][:, :], ps[:, BC_, 0:CK], rs[:, :], ALU.mult).then_inc(S["xn"], 1)

            def shift(m):
                lg = ps[0:TT, BL, 0:G * NE].rearrange("p (g e) -> p g e", e=NE)
                dve.wait_ge(S["lg_mm"], unit("lg_mm", m, 1))
                nc.vector.tensor_reduce(one["mx"][:, :], lg, AX_X, ALU.max).then_inc(S["route"], 1)
                dve.wait_ge(S["route"], unit("route", m, 1))
                nc.vector.tensor_tensor(small["shift"][:, :, :], lg, wide(one["mx"][:, :]), ALU.subtract)\
                    .then_inc(S["shift"], 1)

            def route(m):
                s = {n: a[:, :, :] for n, a in small.items()}
                o = {n: a[:, :] for n, a in one.items()}
                rank = w("rank").rearrange("p (g e) -> p g e", e=NE)
                tt, v = nc.vector.tensor_tensor, nc.vector
                dve.wait_ge(S["e"], unit("e", m, 1))
                v.tensor_reduce(o["sum"], s["e"], AX_X, ALU.add).then_inc(S["route"], 1)
                dve.wait_ge(S["route"], unit("route", m, 2))
                v.reciprocal(o["rsum"], o["sum"]).then_inc(S["route"], 1)
                dve.wait_ge(S["route"], unit("route", m, 3))
                tt(s["p"], s["e"], wide(o["rsum"]), ALU.mult).then_inc(S["route"], 1)
                dve.wait_ge(S["route"], unit("route", m, 4))
                v.tensor_reduce(o["m1"], s["p"], AX_X, ALU.max).then_inc(S["route"], 1)
                dve.wait_ge(S["route"], unit("route", m, 5))
                tt(s["eq1"], s["p"], wide(o["m1"]), ALU.is_ge).then_inc(S["route"], 1)
                dve.wait_ge(S["route"], unit("route", m, 6))
                tt(s["key1"], s["eq1"], rank, ALU.mult).then_inc(S["route"], 1)
                dve.wait_ge(S["route"], unit("route", m, 7))
                v.tensor_reduce(o["k1"], s["key1"], AX_X, ALU.max).then_inc(S["route"], 1)
                dve.wait_ge(S["route"], unit("route", m, 8))
                tt(s["sel1"], rank, wide(o["k1"]), ALU.is_equal).then_inc(S["route"], 1)
                dve.wait_ge(S["route"], unit("route", m, 9))
                v.scalar_tensor_tensor(out=s["rest"], in0=s["sel1"], scalar=-2.0, in1=s["p"], op0=ALU.mult,
                                       op1=ALU.add).then_inc(S["route"], 1)
                dve.wait_ge(S["route"], unit("route", m, 10))
                v.tensor_reduce(o["m2"], s["rest"], AX_X, ALU.max).then_inc(S["route"], 1)
                dve.wait_ge(S["route"], unit("route", m, 11))
                tt(s["eq2"], s["rest"], wide(o["m2"]), ALU.is_ge).then_inc(S["route"], 1)
                tt(o["den"], o["m1"], o["m2"], ALU.add).then_inc(S["route"], 1)
                dve.wait_ge(S["route"], unit("route", m, 13))
                tt(s["key2"], s["eq2"], rank, ALU.mult).then_inc(S["route"], 1)
                v.tensor_scalar(o["den"], o["den"], 1e-12, None, ALU.max).then_inc(S["route"], 1)
                dve.wait_ge(S["route"], unit("route", m, 15))
                v.tensor_reduce(o["k2"], s["key2"], AX_X, ALU.max).then_inc(S["route"], 1)
                v.reciprocal(o["rden"], o["den"]).then_inc(S["route"], 1)
                dve.wait_ge(S["route"], unit("route", m, 17))
                tt(s["sel2"], rank, wide(o["k2"]), ALU.is_equal).then_inc(S["route"], 1)
                dve.wait_ge(S["route"], unit("route", m, 18))
                tt(s["both"], s["sel1"], s["sel2"], ALU.add).then_inc(S["route"], 1)
                dve.wait_ge(S["route"], unit("route", m, 19))
                tt(s["both"], s["both"], s["p"], ALU.mult).then_inc(S["route"], 1)
                dve.wait_ge(S["route"], unit("route", m, 20))
                dve.wait_ge(S["tr_mm"], unit("tr_mm", m, 0))
                tt(s["comb"], s["both"], wide(o["rden"]), ALU.mult).then_inc(S["route"], 1)

            def spread(m, k):
                tr = ps[0:2 * NE, BV, 0:CK]
                c = cparts[k]
                dve.wait_ge(S["tr_mm"], unit("tr_mm", m, 1))
                dve.wait_ge(S["l2_mm"], unit("l2_mm", m - 1, 0))
                nc.vector.tensor_copy(c[0:16, :], tr).then_inc(S["cb_hi"], 1)
                dve.wait_ge(S["cb_hi"], unit("cb_hi", m, 1))
                nc.vector.tensor_tensor(c[32:48, :], tr, hi(c[0:16, :]), ALU.subtract).then_inc(S["cb_mid"], 1)
                dve.wait_ge(S["cb_mid"], unit("cb_mid", m, 1))
                nc.vector.tensor_tensor(c[64:80, :], c[32:48, :], hi(c[32:48, :]), ALU.subtract).then_inc(S["cb_lo"], 1)

            def scale(n, e):
                dve.wait_ge(S["b_mm"], unit("b_mm", n, e + 1))
                dve.wait_ge(S["hid"], unit("hid", n, e + 1))
                dve.wait_ge(S["l2_mm"], unit("l2_mm", n, e - 1))
                nc.vector.tensor_tensor(scaled[e % 2][:, :], ps[:, BB + e % 2, 0:CK], hid[e % 2][:, :], ALU.mult)\
                    .then_inc(S["scaled"], 1)

            def finish(n, k, stores):
                dve.wait_ge(S["l2_mm"], unit("l2_mm", n, 8))
                dve.wait_ge(S["res"], unit("res", n, 1))
                dve.wait_ge(o_out[k], 16 * stores)
                nc.vector.tensor_tensor(osb[k][:, :], ps[:, BO, 0:CK], res[k][:, :], ALU.add).then_inc(S["o_done"], 1)

            dve.wait_ge(ready, 1)
            normalize(0, 0)
            shift(0)
            route(0)
            spread(0, 0)
            with dve.Fori(0, UNITS // 2) as i:
                for k in range(2):
                    n = i * 2 + k
                    for e in range(8):
                        scale(n, e)
                        if e == 1:
                            normalize(n + 1, 1 - k)
                        if e == 3:
                            shift(n + 1)
                        if e == 4:
                            route(n + 1)
                    finish(n, k, i + 1)
                    spread(n + 1, 1 - k)


def pack_weights(a):
    p = np.zeros((128, NW), np.float32)

    def put(name, v):
        at, rows, cols = AT[name]
        p[0:rows, at:at + cols] = np.asarray(v).reshape(rows, cols)

    t = lambda name: a["L0_tok_" + name]
    two = lambda v: np.concatenate([v, v])
    blk = lambda m: np.block([[m, np.zeros_like(m)], [np.zeros_like(m), m]])
    w1 = t("W1").reshape(2, KF, D)
    put("w1T", w1.transpose(2, 0, 1))
    put("w1dup", np.concatenate([w1, w1], axis=2).transpose(1, 0, 2))
    put("ln1g", t("ln1_g").reshape(2, KF).T)
    put("ln1b", t("ln1_b").reshape(2, KF).T)
    for name, key in (("b1", "b1"), ("g2", "ln2_g"), ("be2", "ln2_b"), ("bp1", "bp1"), ("gp", "lnp_g"),
                      ("bep", "lnp_b"), ("bp2", "bp2")):
        put(name, two(t(key)))
    put("wp1", blk(t("Wp1")))
    put("wp1T", blk(t("Wp1").T))
    put("wp2", blk(t("Wp2")))
    put("wp2T", blk(t("Wp2").T))
    put("cen", blk(np.eye(D, dtype=np.float32) - np.float32(1 / D)))
    put("avg", blk(np.full((D, D), 1 / D, np.float32)))
    put("ones1", np.full((KF, KF), 1 / NF, np.float32))
    m = lambda name: [a["L0_attn_f_" + name], a["L0_attn_r_" + name]]
    inw = m("in_w")
    put("inx", two(np.stack([v[0:D].T for v in inw], 1)))
    cw = np.stack([v[:, ::-1].T for v in m("conv_w")], 1)
    put("convw", np.repeat(cw, D, axis=0))
    inz = np.zeros((128, 2, D), np.float32)
    inz[0:D] = np.stack([v[D:2 * D].T for v in inw], 1)
    put("inz", inz)
    put("convb", np.concatenate(m("conv_b")))
    put("dtb", np.concatenate(m("dt_b")))
    put("dvec", np.concatenate(m("D")))
    put("wbc", np.concatenate([np.stack([np.concatenate([v[NR + NS * k:NR + NS * k + NS].T] * DB, 1)
                                         for k in range(2)], 1) for v in m("xproj_w")]))
    wdtr, wdt = np.zeros((128, 32), np.float32), np.zeros((32, 128), np.float32)
    for d in range(2):
        wdtr[D * d:D * d + D, NR * d:NR * d + NR] = m("xproj_w")[d][0:NR].T
        wdt[NR * d:NR * d + NR, D * d:D * d + D] = m("dt_w")[d].T
    put("wdtr", wdtr)
    put("wdt", wdt)
    put("alog", np.stack([v.reshape(NJ, DB * NS) for v in m("A_log")]).reshape(TILES, 128).T)
    wout = np.zeros((128, 2, D), np.float32)
    for d in range(2):
        wout[D * d:D * d + D, d] = m("out_w")[d].T
    put("wout", wout)
    ch = np.arange(128) // NS
    ysel = np.zeros((128, QJ, 32), np.float32)
    selbc = np.zeros((3, 32, QJ, 128), np.float32)
    for j in range(QJ):
        ysel[np.arange(128), j, DB * j + ch] = 1
        selbc[:, DB * j + ch, j, np.arange(128)] = 1
    put("ysel", ysel)
    put("selbc", selbc)
    put("mask8", ch[:, None] == np.arange(DB)[None, :])
    f = lambda name: a["L0_ffn_" + name]
    put("router", blk(f("router_w").T))
    put("ew1", two(f("w1").reshape(4, 2, D, D).transpose(2, 0, 1, 3).reshape(D, 4 * 128)))
    put("eb1", f("b1").reshape(4, 128).T)
    put("ew2", f("w2").reshape(4, 128, D).transpose(1, 0, 2))
    eb2 = np.zeros((2, NE, 2, D), np.float32)
    selcb = np.zeros((80, 2, 4, 128), np.float32)
    for im in range(2):
        eb2[im, :, im] = f("b2")
        for e in range(4):
            for part in range(3):
                for k in range(2):
                    selcb[32 * part + NE * im + 2 * e + k, im, e, D * k:D * k + D] = 1
    put("eb2", eb2)
    put("selcb", selcb)
    put("rank", np.broadcast_to(np.arange(NE, 0, -1, dtype=np.float32), (TT, NTT * 2, NE)))
    put("ident", np.eye(TT, dtype=np.float32))
    return p


def kernel(**inputs):
    import numpy as _np
    import concourse.bacc as _bacc
    from concourse import mybir as _mybir
    from concourse.bass_utils import run_bass_kernel_spmd as _run

    a = {k: _np.asarray(v) for k, v in inputs.items()}
    g = IMG // PATCH
    x = a["x"].reshape(PAIRS, 2, CH, g, PATCH, g, PATCH).transpose(0, 4, 6, 2, 1, 3, 5)
    x = x.reshape(PAIRS, 2, KF, 2, 2, HT).transpose(0, 4, 2, 1, 3, 5)
    nc = _bacc.Bacc("TRN2", target_bir_lowering=False, num_devices=1)
    arrays = {"x_dram": _np.ascontiguousarray(x.reshape(PAIRS, 2, KF, 2, 2 * HT)), "w_dram": pack_weights(a)}
    args = [nc.dram_tensor(n, v.shape, _mybir.dt.from_np(v.dtype), kind="ExternalInput").ap()
            for n, v in arrays.items()]
    out = nc.dram_tensor("out_dram", (PAIRS, 128, L), F32, kind="ExternalOutput").ap()
    vit_tower(nc, *args, out)
    r = _run(nc, [arrays], core_ids=[0])
    got = r.results[0]["out_dram"]
    return _np.ascontiguousarray(got.reshape(B, D, L).transpose(0, 2, 1))
```

```python
import numpy as np

import concourse.bass as bass
from concourse import mybir
from contextlib import ExitStack

F32 = mybir.dt.float32
BF16 = mybir.dt.bfloat16
ALU = mybir.AluOpType
ACT = mybir.ActivationFunctionType
AX_X = mybir.AxisListType.X

B, CH, IMG, PATCH = 16, 3, 224, 8
D = 64
NT = (IMG // PATCH) ** 2
COPIES = 3
L = COPIES * NT
NF = CH * PATCH * PATCH
NS = 16
NR = 16
NE = 8
EPS = 1e-5
PAIRS = B // 2
KF = NF // 2
HT = NT // 2
TC = NT + 1
TP = TC + 1
TH = TP // 2
DB = 8
NJ = D // DB
TILES = 2 * NJ
QJ = 4
NQ = TILES // QJ
CK = 294
NCK = L // CK
TT = 98
NTT = CK // TT

PACK = [
    ("w1T", D, 2 * KF), ("w1dup", KF, 2 * 128), ("ln1g", KF, 2), ("ln1b", KF, 2),
    ("b1", 128, 1), ("g2", 128, 1), ("be2", 128, 1), ("bp1", 128, 1), ("gp", 128, 1), ("bep", 128, 1), ("bp2", 128, 1),
    ("wp1", 128, 128), ("wp1T", 128, 128), ("wp2", 128, 128), ("wp2T", 128, 128),
    ("cen", 128, 128), ("avg", 128, 128), ("ones1", KF, KF),
    ("inx", 128, 2 * D), ("convw", 128, 2 * D), ("inz", 128, 2 * D),
    ("convb", 128, 1), ("dtb", 128, 1), ("dvec", 128, 1), ("wbc", 128, 2 * 128),
    ("wdtr", 128, 32), ("wdt", 32, 128), ("alog", 128, TILES),
    ("ysel", 128, QJ * 32), ("mask8", 128, DB), ("wout", 128, 2 * D),
    ("router", 128, 2 * NE), ("ew1", 128, 4 * 128), ("eb1", 128, 4), ("ew2", 128, 4 * D), ("eb2", 16, 2 * D),
    ("rank", TT, NTT * 4 * NE), ("ident", TT, TT),
    ("selbc", 96, QJ * 128), ("selcb", 80, 8 * 128),
]
AT, NW = {}, 0
for _name, _rows, _cols in PACK:
    AT[_name] = (NW, _rows, _cols)
    NW += _cols


def vit_tower(nc, x, wpack, out):
    with ExitStack() as top:
        def sem(name):
            return top.enter_context(nc.semaphore(name))

        ps = top.enter_context(nc.psum_tensor("ps", [128, 8, 512], F32))
        wsb = top.enter_context(nc.sbuf_tensor("wsb", [128, NW], F32))
        h_d = nc.dram_tensor("h_d", (PAIRS + 1, 128, NT), F32, kind="Internal").ap()
        hn_d = nc.dram_tensor("hn_d", (PAIRS + 1, 128, TP), F32, kind="Internal").ap()
        h2_d = nc.dram_tensor("h2_d", (PAIRS + 2, 128, L), F32, kind="Internal").ap()

        def w(name):
            at, rows, cols = AT[name]
            return wsb[0:rows, at:at + cols]

        def w3(name, n):
            return w(name).rearrange("p (a b) -> p a b", a=n)

        w1c = top.enter_context(nc.sbuf_tensor("w1c", [KF, 2, D], F32))
        wp1g = top.enter_context(nc.sbuf_tensor("wp1g", [128, 128], F32))
        wp2c = top.enter_context(nc.sbuf_tensor("wp2c", [128, 128], F32))
        vecs = top.enter_context(nc.sbuf_tensor("vecs", [128, 8], F32))
        c0c, bp1c, bp2c = vecs[:, 0:1], vecs[:, 1:2], vecs[:, 2:3]
        v_c0, v_bp1, v_eps = vecs[:, 3:4], vecs[:, 4:5], vecs[:, 5:6]
        wconv = top.enter_context(nc.sbuf_tensor("wconv", [128, 2, D], F32))
        aneg = top.enter_context(nc.sbuf_tensor("aneg", [128, TILES], F32))
        selbc = top.enter_context(nc.sbuf_tensor("selbc", [96, QJ, 128], BF16))
        selcb = top.enter_context(nc.sbuf_tensor("selcb", [80, 8, 128], BF16))

        tokenize(nc, ps, sem, w, w3, x, wpack, wsb, h_d, hn_d, h2_d, w1c, wp1g, wp2c,
                 (c0c, bp1c, bp2c, v_c0, v_bp1, v_eps), wconv, aneg, selbc, selcb)
        mamba(nc, ps, sem, w, w3, h_d, hn_d, h2_d, wconv, aneg, selbc)
        experts(nc, ps, sem, w, w3, h2_d, out, selcb, v_eps)


def tokenize(nc, ps, sem, w, w3, x, wpack, wsb, h_d, hn_d, h2_d, w1c, wp1g, wp2c, cols, wconv, aneg, selbc, selcb):
    c0c, bp1c, bp2c, v_c0, v_bp1, v_eps = cols
    with ExitStack() as ctx:
        def sb(name, shape, dt=F32):
            return ctx.enter_context(nc.sbuf_tensor(name, shape, dt))

        zero = sb("zero", [128, L])
        w1g = sb("w1g", [KF, 2, D])
        xin = [sb(f"xin{h}", [KF, 2, 2 * HT]) for h in range(2)]
        xsq = [sb(f"xsq{h}", [KF, 2, 2 * HT]) for h in range(2)]
        unit = {n: [sb(f"{n}{h}", [128, HT]) for h in range(2)] for n in
                ("musq", "var1", "yc", "sq2", "tok", "sq3", "t3", "act", "hs", "sq4",
                 "ln1", "rs1", "ln2", "rs2", "ln3", "rs3", "ln4", "rs4")}
        hns = sb("hns", [128, TP])
        wload, zeroed, zstored = sem("wload"), sem("zeroed"), sem("zstored")
        su_pe, su_act, su_dve, w_ready = sem("su_pe"), sem("su_act"), sem("su_dve"), sem("w_ready")
        TWO = ("rs1", "rs2", "rs3", "rs4", "var1")
        S = {n: [sem(f"t_{n}{h}") for h in range(2)] for n in
             ("x_in", "xsq", "a_mm", "mu_mm", "musq", "q_mm", "yc", "sq2", "var2_mm", "tok", "u_mm", "sq3", "var3_mm",
              "t3", "act", "h_mm", "hs", "sq4", "var4_mm", "hns", "h_out") + TWO}
        hn_out, ends = sem("t_hn_out"), sem("t_ends")
        BY = {n: 16 if n in ("x_in", "h_out") else 2 if n in TWO else 1 for n in S}

        def pair(name, i, c=None):
            k = BY[name]
            return i * k + (2 * k + (k if c is None else c))

        def bank(h, k):
            return ps[:, 4 * h + k, 0:HT]

        def images(h):
            return [(slice(64 * im, 64 * im + 64), slice(HT * im, HT * im + HT)) for im in range(2)]

        def bodies(engine, body):
            with engine.Fori(0, PAIRS - 2) as i:
                body(i, True, True)
            body(PAIRS - 2, True, False)
            body(PAIRS - 1, False, False)

        block = ctx.enter_context(nc.Block())

        @block.gpsimd
        def _(pool):
            for n in S:
                for h in range(2):
                    pool.sem_inc(S[n][h], 2 * BY[n])
            pool.sem_inc(hn_out, 16)

            def squares(i):
                for h in range(2):
                    pool.wait_ge(S["q_mm"][h], pair("q_mm", i, 0))
                    pool.wait_ge(S["x_in"][h], pair("x_in", i))
                    nc.gpsimd.tensor_tensor(xsq[h][:, :, :], xin[h][:, :, :], xin[h][:, :, :], ALU.mult)\
                        .then_inc(S["xsq"][h], 1)

            squares(0)
            squares(1)
            with pool.Fori(0, PAIRS - 2) as i:
                squares(i + 2)

        @block.sync
        def _(sp):
            sp.dma_start(wsb[:, :], wpack).then_inc(wload, 16)

            def load(i):
                for h in range(2):
                    sp.wait_ge(S["a_mm"][h], pair("a_mm", i, 0))
                    sp.wait_ge(S["mu_mm"][h], pair("mu_mm", i, 0))
                    sp.wait_ge(S["xsq"][h], pair("xsq", i, 0))
                    sp.dma_start(xin[h][:, :, :], x[i, h]).then_inc(S["x_in"][h], 16)

            def store(i):
                for h in range(2):
                    sp.wait_ge(S["hs"][h], pair("hs", i))
                    sp.dma_start(h_d[i + 1, :, HT * h:HT * h + HT], unit["hs"][h][:, :]).then_inc(S["h_out"][h], 16)
                sp.wait_ge(ends, i + 1)
                sp.dma_start(hn_d[i], hns[:, :]).then_inc(hn_out, 16)

            load(0)
            load(1)
            sp.wait_ge(zeroed, 1)
            sp.dma_start(h_d[0], zero[:, 0:NT]).then_inc(zstored, 16)
            sp.dma_start(hn_d[PAIRS], zero[:, 0:TP]).then_inc(zstored, 16)
            sp.dma_start(h2_d[PAIRS + 1], zero[:, :]).then_inc(zstored, 16)
            load(2)
            with sp.Fori(0, PAIRS - 3) as i:
                store(i)
                load(i + 3)
            for i in range(PAIRS - 3, PAIRS):
                store(i)
            sp.wait_ge(zstored, 48)
            for h in range(2):
                sp.wait_ge(S["h_out"][h], pair("h_out", PAIRS - 1))
            sp.wait_ge(hn_out, 16 * (PAIRS + 1))

        @block.tensor
        def _(pe):
            pe.wait_ge(wload, 16)
            for c in range(2):
                nc.tensor.matmul(ps[0:KF, c, 0:D], w3("w1T", 2)[:, c, :], w("cen")[0:D, 0:D],
                                 start=True, stop=True).then_inc(su_pe, 1)
            nc.tensor.matmul(ps[:, 2, 0:128], w("wp1T"), w("cen"), start=True, stop=True).then_inc(su_pe, 1)
            nc.tensor.matmul(ps[:, 3, 0:128], w("wp2T"), w("cen"), start=True, stop=True).then_inc(su_pe, 1)
            for c in range(2):
                mm = nc.tensor.matmul(ps[:, 4, 0:1], w3("w1dup", 2)[:, c, :], w3("ln1b", 2)[:, c, :],
                                      start=(c == 0), stop=(c == 1))
            mm.then_inc(su_pe, 1)
            nc.tensor.matmul(ps[:, 5, 0:1], w("wp1"), w("be2"), start=True, stop=True).then_inc(su_pe, 1)
            pe.wait_ge(su_dve, 2)
            for c in range(2):
                mm = nc.tensor.matmul(ps[0:KF, 6, 0:D], w("ones1"), w1g[:, c, :], start=(c == 0), stop=(c == 1))
            mm.then_inc(su_pe, 1)
            pe.wait_ge(su_dve, 5)
            nc.tensor.matmul(ps[:, 7, 0:1], w("cen"), v_c0, start=True, stop=True).then_inc(su_pe, 1)
            nc.tensor.matmul(ps[:, 4, 0:1], w("cen"), v_bp1, start=True, stop=True).then_inc(su_pe, 1)
            nc.tensor.matmul(ps[:, 5, 0:1], w("cen"), w("bp2"), start=True, stop=True).then_inc(su_pe, 1)
            pe.wait_ge(w_ready, 1)

            def mean(i, h):
                pe.wait_ge(S["x_in"][h], pair("x_in", i))
                pe.wait_ge(S["rs2"][h], pair("rs2", i - 1, 1))
                for c in range(2):
                    for rows, toks in images(h):
                        mm = nc.tensor.matmul(bank(h, 1)[rows, :], w("ones1")[:, 0:D], xin[h][:, c, toks],
                                              start=(c == 0), stop=(c == 1))
                mm.then_inc(S["mu_mm"][h], 1)

            def product(i, h):
                pe.wait_ge(S["yc"][h], pair("yc", i, 0))
                for c in range(2):
                    for rows, toks in images(h):
                        mm = nc.tensor.matmul(bank(h, 0)[rows, :], w1c[:, c, :], xin[h][:, c, toks],
                                              start=(c == 0), stop=(c == 1))
                mm.then_inc(S["a_mm"][h], 1)

            def mean_square(i, h):
                pe.wait_ge(S["xsq"][h], pair("xsq", i))
                pe.wait_ge(S["musq"][h], pair("musq", i))
                for c in range(2):
                    for rows, toks in images(h):
                        mm = nc.tensor.matmul(bank(h, 1)[rows, :], w("ones1")[:, 0:D], xsq[h][:, c, toks],
                                              start=(c == 0), stop=(c == 1))
                mm.then_inc(S["q_mm"][h], 1)

            def variance(i, h, k):
                if k == 2:
                    pe.wait_ge(S["var1"][h], pair("var1", i, 1))
                if k == 3:
                    pe.wait_ge(S["rs4"][h], pair("rs4", i - 1, 1))
                if k == 4:
                    pe.wait_ge(S["hs"][h], pair("hs", i))
                sq = f"sq{k}"
                pe.wait_ge(S[sq][h], pair(sq, i))
                nc.tensor.matmul(bank(h, 1 if k == 2 else 3), w("avg"), unit[sq][h][:, :], start=True, stop=True)\
                    .then_inc(S[f"var{k}_mm"][h], 1)

            def hidden(i, h):
                pe.wait_ge(S["hns"][h], pair("hns", i, 0))
                pe.wait_ge(S["tok"][h], pair("tok", i))
                nc.tensor.matmul(bank(h, 2), wp1g[:, :], unit["tok"][h][:, :], start=True, stop=True)\
                    .then_inc(S["u_mm"][h], 1)

            def tokens(i, h):
                pe.wait_ge(S["act"][h], pair("act", i))
                nc.tensor.matmul(bank(h, 2), wp2c[:, :], unit["act"][h][:, :], start=True, stop=True)
                nc.tensor.matmul(bank(h, 3), w("wp2"), unit["act"][h][:, :], start=True, stop=True)\
                    .then_inc(S["h_mm"][h], 1)

            def stage_a(i):
                for h in range(2):
                    mean(i, h)
                for h in range(2):
                    product(i, h)
                for h in range(2):
                    mean_square(i, h)

            def body(i, stage_b, with_a):
                for h in range(2):
                    tokens(i, h)
                for h in range(2):
                    variance(i, h, 4)
                    if stage_b:
                        variance(i + 1, h, 2)
                if with_a:
                    for h in range(2):
                        mean(i + 2, h)
                if stage_b:
                    for h in range(2):
                        hidden(i + 1, h)
                if with_a:
                    for h in range(2):
                        product(i + 2, h)
                if stage_b:
                    for h in range(2):
                        variance(i + 1, h, 3)
                if with_a:
                    for h in range(2):
                        mean_square(i + 2, h)

            stage_a(0)
            for h in range(2):
                variance(0, h, 2)
            for h in range(2):
                hidden(0, h)
            for h in range(2):
                variance(0, h, 3)
            stage_a(1)
            bodies(pe, body)

        @block.scalar
        def _(act):
            act.wait_ge(wload, 16)
            nc.scalar.activation(aneg[:, :], w("alog"), ACT.Exp).then_inc(su_act, 1)
            act.wait_ge(w_ready, 1)

            def square(i, h, name, produced, src, bias=0.0):
                act.wait_ge(S[produced][h], pair(produced, i))
                nc.scalar.activation(unit[name][h][:, :], src, ACT.Square, bias=bias).then_inc(S[name][h], 1)

            def norm(i, k, produced, src):
                rs, ln = f"rs{k}", f"ln{k}"
                for h in range(2):
                    act.wait_ge(S[produced][h], pair(produced, i))
                    nc.scalar.activation(unit[ln][h][:, :], src(h), ACT.Ln, bias=v_eps).then_inc(S[rs][h], 1)
                for h in range(2):
                    act.wait_ge(S[rs][h], pair(rs, i, 1))
                    nc.scalar.activation(unit[rs][h][:, :], unit[ln][h][:, :], ACT.Exp, scale=-0.5)\
                        .then_inc(S[rs][h], 1)

            def mean_squared(i):
                for h in range(2):
                    square(i, h, "musq", "mu_mm", bank(h, 1))

            def first_norm(i):
                norm(i, 1, "var1", lambda h: unit["var1"][h][:, :])

            def second_norm(i):
                norm(i, 2, "var2_mm", lambda h: bank(h, 1))

            def third_norm(i):
                for h in range(2):
                    square(i, h, "sq3", "u_mm", bank(h, 2), bp1c)
                norm(i, 3, "var3_mm", lambda h: bank(h, 3))

            def body(i, stage_b, with_a):
                for h in range(2):
                    act.wait_ge(S["t3"][h], pair("t3", i))
                    nc.scalar.activation(unit["act"][h][:, :], unit["t3"][h][:, :], ACT.Silu, bias=w("bep"),
                                         scale=w("gp")).then_inc(S["act"][h], 1)
                nc.scalar.preload_act_table_set("natural_log_exp_and_others")
                if stage_b:
                    first_norm(i + 1)
                for h in range(2):
                    act.wait_ge(S["h_out"][h], pair("h_out", i, 0))
                    act.wait_ge(S["h_mm"][h], pair("h_mm", i))
                    nc.scalar.activation(unit["hs"][h][:, :], bank(h, 3), ACT.Identity, bias=w("bp2"))\
                        .then_inc(S["hs"][h], 1)
                    square(i, h, "sq4", "h_mm", bank(h, 2), bp2c)
                if stage_b:
                    for h in range(2):
                        square(i + 1, h, "sq2", "yc", unit["yc"][h][:, :], c0c)
                norm(i, 4, "var4_mm", lambda h: bank(h, 3))
                if stage_b:
                    second_norm(i + 1)
                if with_a:
                    mean_squared(i + 2)
                if stage_b:
                    third_norm(i + 1)

            nc.scalar.preload_act_table_set("natural_log_exp_and_others")
            mean_squared(0)
            first_norm(0)
            for h in range(2):
                square(0, h, "sq2", "yc", unit["yc"][h][:, :], c0c)
            second_norm(0)
            third_norm(0)
            mean_squared(1)
            bodies(act, body)

        @block.vector
        def _(dve):
            nc.vector.memset(zero[:, :], 0.0).then_inc(zeroed, 1)
            nc.vector.memset(v_eps, EPS)
            dve.wait_ge(wload, 16)
            dve.wait_ge(su_pe, 2)
            for c in range(2):
                nc.vector.tensor_scalar(w1g[:, c, :], ps[0:KF, c, 0:D], w3("ln1g", 2)[:, c, :], None, ALU.mult)\
                    .then_inc(su_dve, 1)
            dve.wait_ge(su_pe, 6)
            nc.vector.tensor_tensor(v_c0, ps[:, 4, 0:1], w("b1"), ALU.add).then_inc(su_dve, 1)
            nc.vector.tensor_tensor(v_bp1, ps[:, 5, 0:1], w("bp1"), ALU.add).then_inc(su_dve, 1)
            nc.vector.tensor_scalar(wp1g[:, :], ps[:, 2, 0:128], w("g2"), None, ALU.mult).then_inc(su_dve, 1)
            nc.vector.tensor_copy(wp2c[:, :], ps[:, 3, 0:128])
            nc.vector.tensor_tensor(wconv[:, :, :].rearrange("p a b -> p (a b)"), w("inx"), w("convw"), ALU.mult)
            nc.vector.tensor_copy(selbc[:, :, :].rearrange("p a b -> p (a b)"), w("selbc"))
            nc.vector.tensor_copy(selcb[:, :, :].rearrange("p a b -> p (a b)"), w("selcb"))
            dve.wait_ge(su_act, 1)
            nc.vector.tensor_scalar(aneg[:, :], aneg[:, :], -1.0, None, ALU.mult)
            dve.wait_ge(su_pe, 7)
            for c in range(2):
                nc.vector.tensor_tensor(w1c[:, c, :], w1g[:, c, :], ps[0:KF, 6, 0:D], ALU.subtract)
            dve.wait_ge(su_pe, 10)
            nc.vector.tensor_copy(c0c, ps[:, 7, 0:1])
            nc.vector.tensor_copy(bp1c, ps[:, 4, 0:1])
            nc.vector.tensor_copy(bp2c, ps[:, 5, 0:1])
            nc.vector.drain().then_inc(w_ready, 1)

            def first_variance(i):
                for h in range(2):
                    dve.wait_ge(S["rs1"][h], pair("rs1", i, 0))
                    dve.wait_ge(S["q_mm"][h], pair("q_mm", i))
                    nc.vector.tensor_tensor(unit["var1"][h][:, :], bank(h, 1), unit["musq"][h][:, :], ALU.subtract)\
                        .then_inc(S["var1"][h], 1)
                for h in range(2):
                    dve.wait_ge(S["var1"][h], pair("var1", i, 1))
                    nc.vector.tensor_scalar(unit["var1"][h][:, :], unit["var1"][h][:, :], 0.0, None, ALU.max)\
                        .then_inc(S["var1"][h], 1)

            def first_norm(i):
                for h in range(2):
                    dve.wait_ge(S["a_mm"][h], pair("a_mm", i))
                    dve.wait_ge(S["rs1"][h], pair("rs1", i))
                    nc.vector.tensor_tensor(unit["yc"][h][:, :], bank(h, 0), unit["rs1"][h][:, :], ALU.mult)\
                        .then_inc(S["yc"][h], 1)

            def norm(i, h, name, src, bias, rs, dst):
                dve.wait_ge(S[rs][h], pair(rs, i))
                nc.vector.scalar_tensor_tensor(out=dst, in0=src, scalar=bias, in1=unit[rs][h][:, :],
                                               op0=ALU.add, op1=ALU.mult).then_inc(S[name][h], 1)

            def second_norm(i):
                for h in range(2):
                    norm(i, h, "tok", unit["yc"][h][:, :], c0c, "rs2", unit["tok"][h][:, :])

            def third_norm(i):
                for h in range(2):
                    norm(i, h, "t3", bank(h, 2), bp1c, "rs3", unit["t3"][h][:, :])

            def body(i, stage_b, with_a):
                if stage_b:
                    first_norm(i + 1)
                dve.wait_ge(hn_out, i * 16 + 16)
                for h in range(2):
                    norm(i, h, "hns", bank(h, 2), bp2c, "rs4", hns[:, HT * h + 1:HT * h + 1 + HT])
                for h in range(2):
                    dve.wait_ge(S["hns"][h], pair("hns", i))
                nc.vector.tensor_copy(hns[:, 0:1], hns[:, NT:NT + 1])
                nc.vector.tensor_copy(hns[:, NT + 1:NT + 2], hns[:, 1:2]).then_inc(ends, 1)
                if stage_b:
                    second_norm(i + 1)
                    third_norm(i + 1)
                if with_a:
                    first_variance(i + 2)

            first_variance(0)
            first_norm(0)
            second_norm(0)
            third_norm(0)
            first_variance(1)
            bodies(dve, body)


def mamba(nc, ps, sem, w, w3, h_d, hn_d, h2_d, wconv, aneg, selbc):
    with ExitStack() as ctx:
        def sb(name, shape, dt=F32):
            return ctx.enter_context(nc.sbuf_tensor(name, shape, dt))

        hf = sb("hf", [128, TP])
        hb = sb("hb", [128, TP])
        hres = sb("hres", [128, NT])
        xc = [sb(f"xc{k}", [128, TP]) for k in range(2)]
        gate = [sb(f"gate{k}", [128, TP]) for k in range(2)]
        bcs = [sb(f"bcs{k}", [128, 2, 2, TP]) for k in range(2)]
        dtr = sb("dtr", [32, TP])
        parts = [sb(f"parts{k}", [128, 3, TP]) for k in range(3)]
        stack = sb("stack", [96, NQ, 3, TP])
        da, dbx, hs, ch, pc, cp = ([sb(f"{n}{k}", [128, TP]) for k in range(2)]
                                   for n in ("da", "dbx", "hst", "chs", "pcum", "cps"))
        delta = sb("delta", [128, 2, 2])
        wdel = sb("wdel", [128, QJ, 2, 32])
        yall = sb("yall", [128, 3, TP])
        fin = sb("fin", [128, L + 1])
        osb = [sb(f"osb{k}", [128, HT]) for k in range(2)]
        ones = sb("ones", [128, 1])

        per_tile = ("dt_bc", "u_bc", "s_bc", "da_done", "p_done", "dbx_done", "scan_done", "ch_done", "del_done",
                    "del2_done", "wdel_done", "cp_done", "y_mm", "w_mm")
        per_image = dict(conv_mm=2, xc_done=2, z_mm=2, g_done=2, dtr_mm=2, dtr_done=2, dt_mm=2, pre_done=2,
                         abs_done=1, relu_done=1, e_done=1, ln_done=1, r_done=1, sum_done=1, c_done=1, dt_done=1,
                         bc_mm=8, bc_done=8, s_done=1, u_done=1, r1_done=1, r2_done=1, yd_done=1, e0_done=1, wg_done=2,
                         f_done=2, out_mm=6, out_done=6, evac=12, hres_in=16)
        T = {n: sem("m_" + n) for n in per_tile}
        S = {n: sem("m_" + n) for n in per_image}
        stk = [sem(f"m_stk{q}") for q in range(NQ)]
        q_used = [sem(f"m_q_used{q}") for q in range(NQ)]
        hfb_in, stored, ready = sem("hfb_in"), [sem(f"h2_stored{k}") for k in range(2)], sem("m_ready")
        READY = 2

        def tile(n, t):
            return n * TILES + (t + 3)

        def img(name, n, c):
            k = per_image[name]
            return n * k + (k + c)

        BX, BU, BY, BG = 0, 2, 4, 6

        def halves(bank):
            return ps[:, bank:bank + 2, 0:TH]

        def two(ap):
            return ap.rearrange("p (a b) -> p a b", a=2)

        def hi(ap):
            return ap.bitcast(BF16)[..., 1::2]

        block = ctx.enter_context(nc.Block())

        @block.sync
        def _(sp):
            def load_hn(pair, im):
                rows = slice(64 * im, 64 * im + 64)
                sp.dma_start(hf[0:64, 0:TC], hn_d[pair, rows, 1:TP]).then_inc(hfb_in, 16)
                sp.dma_start(hf[64:128, 1:TC], hn_d[pair, rows, 1:TC]).then_inc(hfb_in, 16)
                sp.dma_start(hb[0:64, 0:TC], hn_d[pair, rows, 0:TC]).then_inc(hfb_in, 16)
                sp.dma_start(hb[64:128, 0:NT], hn_d[pair, rows, 1:TC]).then_inc(hfb_in, 16)

            def restack(m, quarters):
                nth = img("r2_done", m, 1)
                if type(m) is not int:
                    nth = sp.snap(nth)
                if 0 in quarters:
                    sp.wait_ge(S["r2_done"], nth)
                for q in quarters:
                    if type(m) is not int:
                        sp.wait_ge(q_used[q], nth)
                    for k in range(3):
                        sp.dma_start(stack[32 * k:32 * k + 32, q, :, :], parts[k][32 * q:32 * q + 32, :, :])\
                            .then_inc(stk[q], 16)

            sp.wait_ge(ready, READY)
            load_hn(0, 0)
            restack(0, range(NQ))

            with sp.Fori(0, PAIRS) as i:
                following = sp.snap(i + 1)
                for par in range(2):
                    n = i * 2 + par
                    sp.wait_ge(S["z_mm"], img("z_mm", n, 2))
                    load_hn(i if par == 0 else following, 1 - par)
                    im = slice(64 * (1 - par), 64 * (1 - par) + 64)
                    sp.wait_ge(S["out_done"], img("out_done", n, 0))
                    sp.dma_start(hres[im, :], h_d[i + par, im, :]).then_inc(S["hres_in"], 16)
                    restack(n + 1, range(NQ - 1))
                    for c in range(6):
                        sp.wait_ge(S["out_done"], img("out_done", n, c + 1))
                        sp.dma_start(h2_d[i + par, im, HT * c:HT * c + HT], osb[c % 2][im, :])\
                            .then_inc(stored[c % 2], 16)
                    restack(n + 1, (NQ - 1,))
            im = slice(64, 128)
            sp.wait_ge(S["out_done"], img("out_done", B, 0))
            sp.dma_start(hres[im, :], h_d[PAIRS, im, :]).then_inc(S["hres_in"], 16)
            for c in range(6):
                sp.wait_ge(S["out_done"], img("out_done", B, c + 1))
                sp.dma_start(h2_d[PAIRS, im, HT * c:HT * c + HT], osb[c % 2][im, :]).then_inc(stored[c % 2], 16)
            for k in range(2):
                sp.wait_ge(stored[k], 16 + 16 * 3 * (B + 1))

        @block.gpsimd
        def _(pool):
            for n in per_tile:
                pool.sem_inc(T[n], 2)
            for n, k in per_image.items():
                pool.sem_inc(S[n], k)
            for q in range(NQ):
                pool.sem_inc(stk[q], 48)
                pool.sem_inc(q_used[q], 2)
            for k in range(2):
                pool.sem_inc(stored[k], 16)
            pool.sem_inc(hfb_in, 64)
            nc.gpsimd.memset(wdel[:, :, :, :], 0.0)
            nc.gpsimd.memset(yall[:, :, :], 0.0)
            for k in range(2):
                nc.gpsimd.memset(gate[k][:, :], 0.0)
            nc.gpsimd.drain().then_inc(ready, 1)
            pool.wait_ge(ready, READY)

            def prepare_u(m, k):
                pool.wait_ge(S["dt_done"], img("dt_done", m, 1))
                pool.wait_ge(S["xc_done"], img("xc_done", m, 2))
                nc.gpsimd.tensor_tensor(parts[0][:, 2, 0:TC], parts[0][:, 0, 0:TC], xc[k][:, 0:TC], ALU.mult)\
                    .then_inc(S["u_done"], 1)

            def split(m, k):
                if k == 0:
                    pool.wait_ge(S["s_done"], img("s_done", m, 1))
                    pool.wait_ge(S["u_done"], img("u_done", m, 1))
                else:
                    pool.wait_ge(S["r1_done"], img("r1_done", m, 1))
                name = ("r1_done", "r2_done")[k]
                for v in range(3):
                    op = nc.gpsimd.tensor_tensor(parts[k + 1][:, v, 0:TC], parts[k][:, v, 0:TC],
                                                 hi(parts[k][:, v, 0:TC]), ALU.subtract)
                op.then_inc(S[name], 1)

            def finish(n, k, step):
                g = gate[k]
                if step == 0:
                    pool.wait_ge(S["yd_done"], img("yd_done", n, 1))
                    pool.wait_ge(S["out_mm"], img("out_mm", n, 0))
                    nc.gpsimd.tensor_tensor(fin[:, 0:TC], yall[:, 0, 0:TC], g[:, 0:TC], ALU.mult)\
                        .then_inc(S["e0_done"], 1)
                else:
                    at = TC + NT * (step - 1)
                    nc.gpsimd.tensor_tensor(yall[:, step, 1:TC], yall[:, step, 1:TC], g[:, 1:TC], ALU.mult)\
                        .then_inc(S["wg_done"], 1)
                    pool.wait_ge(S["e0_done"], img("e0_done", n, 1))
                    pool.wait_ge(S["wg_done"], img("wg_done", n, step))
                    nc.gpsimd.tensor_tensor(fin[:, at:at + NT], yall[:, step, 1:TC], fin[:, 1:TC], ALU.add)\
                        .then_inc(S["f_done"], 1)

            prepare_u(0, 0)
            split(0, 0)
            split(0, 1)
            with pool.Fori(0, PAIRS) as i:
                for par in range(2):
                    n = i * 2 + par
                    for t in range(TILES):
                        k, d = t % 2, t // NJ
                        pool.wait_ge(T["p_done"], tile(n, t))
                        pool.wait_ge(T["w_mm"], tile(n, t - 2))
                        nc.gpsimd.tensor_tensor(cp[k][:, 0:TC], pc[k][:, 0:TC], bcs[par][:, d, 1, 0:TC], ALU.mult)\
                            .then_inc(T["cp_done"], 1)
                        if t < 3:
                            finish(n, 1 - par, t)
                        if t == 7:
                            prepare_u(n + 1, 1 - par)
                        if t in (8, 10):
                            split(n + 1, (t - 8) // 2)
            for step in range(3):
                finish(B, 1, step)

        @block.tensor
        def _(pe):
            def bc(bank, q, j, v, name):
                for a in range(2):
                    mm = nc.tensor.matmul(ps[:, bank + a, 0:TH], selbc[:, j, :],
                                          hi(stack[:, q, v, :])[:, TH * a:TH * a + TH], start=True, stop=True)
                mm.then_inc(T[name], 1)

            def ahead(n, t):
                q, j = t // QJ, t % QJ
                if j == 0:
                    pe.wait_ge(stk[q], n * 48 + 96)
                pe.wait_ge(T["p_done"], tile(n, t - 1))
                bc(BX, q, j, 0, "dt_bc")
                pe.wait_ge(T["dbx_done"], tile(n, t - 1))
                bc(BU, q, j, 2, "u_bc")

            def ahead_s(n, t):
                pe.wait_ge(T["da_done"], tile(n, t))
                bc(BX, t // QJ, t % QJ, 1, "s_bc")

            def rows_of(d, f, size):
                return hf[:, f:f + size] if d == 0 else hb[:, NT - f::-1][:, 0:size]

            def conv(m):
                pe.wait_ge(hfb_in, m * 64 + 128)
                pe.wait_ge(S["out_done"], img("out_done", m, -6 if type(m) is not int else 0))
                pe.wait_ge(S["bc_done"], img("bc_done", m, 0))
                for a in range(2):
                    for d in range(2):
                        mm = nc.tensor.matmul(ps[64 * d:64 * d + 64, BG + a, 0:TH - a], wconv[:, d, :],
                                              rows_of(d, TH * a, TH - a), start=True, stop=True)
                    mm.then_inc(S["conv_mm"], 1)

            def gates(m):
                for a in range(2):
                    pe.wait_ge(S["pre_done"], img("pre_done", m, a + 1))
                    for d in range(2):
                        mm = nc.tensor.matmul(ps[64 * d:64 * d + 64, BG + a, 0:TH - a], w3("inz", 2)[:, d, :],
                                              rows_of(d, TH * a, TH - a), start=True, stop=True)
                    mm.then_inc(S["z_mm"], 1)

            def dt_low(m, k):
                for a in range(2):
                    pe.wait_ge(S["xc_done"], img("xc_done", m, a + 1))
                    nc.tensor.matmul(ps[0:32, BG + a, 0:TH], w("wdtr"), xc[k][:, TH * a:TH * a + TH],
                                     start=True, stop=True).then_inc(S["dtr_mm"], 1)

            def dt_full(m):
                for a in range(2):
                    pe.wait_ge(S["dtr_done"], img("dtr_done", m, a + 1))
                    nc.tensor.matmul(ps[:, BG + a, 0:TH], w("wdt"), dtr[:, TH * a:TH * a + TH],
                                     start=True, stop=True).then_inc(S["dt_mm"], 1)

            def b_or_c(m, k, step):
                d, which = step // 2, step % 2
                for a in range(2):
                    if step == 0:
                        pe.wait_ge(S["g_done"], img("g_done", m, a + 1))
                    else:
                        pe.wait_ge(S["bc_done"], img("bc_done", m, 2 * step - 1 + a))
                    nc.tensor.matmul(ps[:, BG + a, 0:TH], w3("wbc", 2)[64 * d:64 * d + 64, which, :],
                                     xc[k][64 * d:64 * d + 64, TH * a:TH * a + TH], start=True, stop=True)\
                        .then_inc(S["bc_mm"], 1)

            def project(n, im, c, before):
                wout = w3("wout", 2)
                if c == 0:
                    pe.wait_ge(S["f_done"], img("f_done", n, 2))
                if c < 2:
                    pe.wait_ge(S["bc_done"], before + c)
                else:
                    pe.wait_ge(S["out_done"], img("out_done", n, c - 1))
                lo = HT * c
                rev = fin[:, L - 1 - lo:L - 1 - lo - HT:-1] if L - 1 - lo - HT >= 0 else fin[:, L - 1 - lo::-1]
                o = ps[64 * im:64 * im + 64, BG + c % 2, 0:HT]
                nc.tensor.matmul(o, wout[:, 0, :], fin[:, lo:lo + HT], start=True, stop=False)
                nc.tensor.matmul(o, wout[:, 1, :], rev, start=False, stop=True).then_inc(S["out_mm"], 1)

            pe.wait_ge(ready, READY)
            conv(0)
            dt_low(0, 0)
            dt_full(0)
            gates(0)
            for step in range(4):
                b_or_c(0, 0, step)
            ahead(0, 0)
            ahead_s(0, 0)
            with pe.Fori(0, PAIRS) as i:
                for par in range(2):
                    n = i * 2 + par
                    for t in range(TILES):
                        nn, tt = (n, t + 1) if t + 1 < TILES else (n + 1, 0)
                        ahead(nn, tt)
                        if t == 1:
                            conv(n + 1)
                        if t == 2:
                            dt_low(n + 1, 1 - par)
                        if t == 3:
                            dt_full(n + 1)
                        if t == 7:
                            gates(n + 1)
                        if 8 <= t < 12:
                            b_or_c(n + 1, 1 - par, t - 8)
                        if 12 <= t < 15:
                            for c in (2 * (t - 12), 2 * (t - 12) + 1):
                                project(n, 1 - par, c, img("bc_done", n + 1, 7))
                        ahead_s(nn, tt)
                        k, j = t % 2, t % QJ
                        pe.wait_ge(T["ch_done"], tile(n, t))
                        if j == 0:
                            pe.wait_ge(S["evac"], img("evac", n, 3 * (t // QJ) - 2))
                        for a in range(2):
                            mm = nc.tensor.matmul(ps[0:32, BY + a, 0:TH - a], w3("ysel", QJ)[:, j, :],
                                                  ch[k][:, TH * a:TH * a + TH - a], start=(j == 0), stop=(j == QJ - 1))
                            if a == 0 and j == QJ - 2:
                                mm.then_inc(q_used[t // QJ], 1)
                        mm.then_inc(T["y_mm"], 1)
                        pe.wait_ge(T["cp_done"], tile(n, t))
                        pe.wait_ge(T["wdel_done"], tile(n, t))
                        if j == 0:
                            pe.wait_ge(S["evac"], img("evac", n, 3 * (t // QJ)))
                        for a in range(2):
                            mm = nc.tensor.matmul(ps[64:128, BY + a, 0:TH - a],
                                                  wdel[:, j, :, :].rearrange("p a b -> p (a b)"),
                                                  cp[k][:, TH * a:TH * a + TH - a], start=(j == 0), stop=(j == QJ - 1))
                        mm.then_inc(T["w_mm"], 1)
            for c in range(6):
                project(B, 1, c, img("bc_done", B, 7))

        @block.scalar
        def _(act):
            def decay(n, t):
                k = t % 2
                act.wait_ge(T["dt_bc"], tile(n, t))
                act.wait_ge(T["scan_done"], tile(n, t - 2))
                nc.scalar.activation(two(da[k][:, :]), halves(BX), ACT.Exp, scale=aneg[:, t:t + 1])\
                    .then_inc(T["da_done"], 1)

            def decay_from_start(n, t):
                k = t % 2
                act.wait_ge(T["s_bc"], tile(n, t))
                act.wait_ge(T["cp_done"], tile(n, t - 2))
                act.wait_ge(T["del2_done"], tile(n, t - 2))
                nc.scalar.activation(two(pc[k][:, :]), halves(BX), ACT.Exp, scale=aneg[:, t:t + 1])\
                    .then_inc(T["p_done"], 1)

            def convolved(m, k):
                if type(m) is not int:
                    act.wait_ge(S["yd_done"], img("yd_done", m, 0))
                act.wait_ge(S["bc_mm"], img("bc_mm", m, 0))
                act.wait_ge(S["u_done"], img("u_done", m, 0))
                for a in range(2):
                    act.wait_ge(S["conv_mm"], img("conv_mm", m, a + 1))
                    nc.scalar.activation(xc[k][:, TH * a:TH * a + TH - a], ps[:, BG + a, 0:TH - a], ACT.Silu,
                                         bias=w("convb")).then_inc(S["xc_done"], 1)

            def gated(m, k):
                if type(m) is not int:
                    act.wait_ge(S["wg_done"], img("wg_done", m, 0))
                    act.wait_ge(S["e0_done"], img("e0_done", m, 0))
                for a in range(2):
                    act.wait_ge(S["z_mm"], img("z_mm", m, a + 1))
                    nc.scalar.activation(gate[k][:, TH * a:TH * a + TH - a], ps[:, BG + a, 0:TH - a], ACT.Silu)\
                        .then_inc(S["g_done"], 1)

            def low(m):
                act.wait_ge(S["dt_mm"], img("dt_mm", m, 0))
                for a in range(2):
                    act.wait_ge(S["dtr_mm"], img("dtr_mm", m, a + 1))
                    nc.scalar.activation(dtr[:, TH * a:TH * a + TH], ps[0:32, BG + a, 0:TH], ACT.Copy)\
                        .then_inc(S["dtr_done"], 1)

            def soft(m):
                for q in range(NQ):
                    act.wait_ge(stk[q], m * 48 + 48)
                for a in range(2):
                    act.wait_ge(S["dt_mm"], img("dt_mm", m, a + 1))
                    nc.scalar.activation(parts[0][:, 0, TH * a:TH * a + TH - a], ps[:, BG + a, 0:TH - a], ACT.Identity,
                                         bias=w("dtb")).then_inc(S["pre_done"], 1)
                act.wait_ge(S["pre_done"], img("pre_done", m, 2))
                nc.scalar.activation(parts[1][:, 0, 0:TC], parts[0][:, 0, 0:TC], ACT.Abs).then_inc(S["abs_done"], 1)

            def soft_exp(m):
                act.wait_ge(S["abs_done"], img("abs_done", m, 1))
                nc.scalar.activation(parts[1][:, 0, 0:TC], parts[1][:, 0, 0:TC], ACT.Exp, scale=-1.0)\
                    .then_inc(S["e_done"], 1)

            def soft_log(m):
                act.wait_ge(S["e_done"], img("e_done", m, 1))
                nc.scalar.activation(parts[2][:, 0, 0:TC], parts[1][:, 0, 0:TC], ACT.Ln, bias=ones[:, :])\
                    .then_inc(S["ln_done"], 1)

            def b_or_c(m, k, step):
                for a in range(2):
                    act.wait_ge(S["bc_mm"], img("bc_mm", m, 2 * step + a + 1))
                    nc.scalar.activation(bcs[k][:, step // 2, step % 2, TH * a:TH * a + TH], ps[:, BG + a, 0:TH],
                                         ACT.Copy).then_inc(S["bc_done"], 1)

            def evacuate(n, q, k):
                rows = (slice(0, 32), slice(64, 96), slice(96, 128))[k]
                if k == 0:
                    act.wait_ge(S["f_done"], img("f_done", n, 2))
                    act.wait_ge(T["y_mm"], tile(n, QJ * q + QJ - 1))
                else:
                    act.wait_ge(T["w_mm"], tile(n, QJ * q + QJ - 1))
                for a in range(2):
                    op = nc.scalar.activation(yall[32 * q:32 * q + 32, k, TH * a:TH * a + TH - a],
                                              ps[rows, BY + a, 0:TH - a], ACT.Copy)
                op.then_inc(S["evac"], 1)

            act.wait_ge(ready, READY)
            convolved(0, 0)
            low(0)
            soft(0)
            gated(0, 0)
            nc.scalar.preload_act_table_set("natural_log_exp_and_others")
            soft_exp(0)
            soft_log(0)
            for step in range(4):
                b_or_c(0, 0, step)
            decay(0, 0)
            decay_from_start(0, 0)
            with act.Fori(0, PAIRS) as i:
                for par in range(2):
                    n = i * 2 + par
                    for t in range(TILES):
                        nn, tt = (n, t + 1) if t + 1 < TILES else (n + 1, 0)
                        spare = t % QJ == 0 and t > 0
                        decay(nn, tt)
                        decay_from_start(nn, tt)
                        if spare:
                            evacuate(n, t // QJ - 1, 2)
                        if t == 1:
                            convolved(n + 1, 1 - par)
                        if t == 2:
                            low(n + 1)
                        if t == 3:
                            soft(n + 1)
                        if t == 7:
                            gated(n + 1, 1 - par)
                        if t in (1, 7):
                            nc.scalar.preload_act_table_set("natural_log_exp_and_others")
                        if t == 4:
                            soft_exp(n + 1)
                        if t == 5:
                            soft_log(n + 1)
                        if 8 <= t < 12:
                            b_or_c(n + 1, 1 - par, t - 8)
                        if t % QJ == QJ - 1:
                            evacuate(n, t // QJ, 0)
                            evacuate(n, t // QJ, 1)
                        if t == TILES - 1:
                            evacuate(n, NQ - 1, 2)

        @block.vector
        def _(dve):
            nc.vector.memset(ones[:, :], 1.0)
            nc.vector.memset(hf[64:128, 0:1], 0.0)
            nc.vector.memset(hb[64:128, NT:TC], 0.0)
            for k in range(2):
                nc.vector.memset(xc[k][:, :], 0.0)
            for k in range(3):
                nc.vector.memset(parts[k][:, :, TC:TP], 0.0)
            nc.vector.memset(parts[0][:, 1, 0:1], 0.0)
            nc.vector.drain().then_inc(ready, 1)
            dve.wait_ge(ready, READY)

            def softplus(m, part):
                e, lost = parts[1][:, 0, 0:TC], parts[1][:, 1, 0:TC]
                total = parts[2][:, 0, 0:TC]
                if part == 0:
                    dve.wait_ge(S["abs_done"], img("abs_done", m, 1))
                    nc.vector.tensor_scalar(parts[0][:, 0, 0:TC], parts[0][:, 0, 0:TC], 0.0, None, ALU.max)\
                        .then_inc(S["relu_done"], 1)
                if part == 1:
                    dve.wait_ge(S["e_done"], img("e_done", m, 1))
                    nc.vector.tensor_scalar(lost, e, 1.0, -1.0, ALU.add, ALU.add).then_inc(S["r_done"], 1)
                    dve.wait_ge(S["r_done"], img("r_done", m, 1))
                    nc.vector.tensor_tensor(lost, e, lost, ALU.subtract).then_inc(S["c_done"], 1)
                if part == 2:
                    dve.wait_ge(S["relu_done"], img("relu_done", m, 1))
                    dve.wait_ge(S["ln_done"], img("ln_done", m, 1))
                    nc.vector.tensor_tensor(total, total, parts[0][:, 0, 0:TC], ALU.add).then_inc(S["sum_done"], 1)
                    dve.wait_ge(S["c_done"], img("c_done", m, 1))
                    dve.wait_ge(S["sum_done"], img("sum_done", m, 1))
                    nc.vector.tensor_tensor(parts[0][:, 0, 0:TC], total, lost, ALU.add).then_inc(S["dt_done"], 1)

            def cumsum(m):
                dve.wait_ge(S["dt_done"], img("dt_done", m, 1))
                nc.vector.tensor_tensor_scan(parts[0][:, 1, 1:TC], ones[:, :].to_broadcast([128, NT]),
                                             parts[0][:, 0, 1:TC], 0.0, ALU.mult, ALU.add).then_inc(S["s_done"], 1)

            def skip_add(n, k):
                dve.wait_ge(S["evac"], img("evac", n, 0))
                nc.vector.scalar_tensor_tensor(out=yall[:, 0, 0:TC], in0=xc[k][:, 0:TC], scalar=w("dvec"),
                                               in1=yall[:, 0, 0:TC], op0=ALU.mult, op1=ALU.add)\
                    .then_inc(S["yd_done"], 1)

            def add_residual(n, im, c):
                rows = slice(64 * im, 64 * im + 64)
                if c == 0:
                    dve.wait_ge(S["hres_in"], img("hres_in", n, 16))
                dve.wait_ge(S["out_mm"], img("out_mm", n, c + 1))
                dve.wait_ge(stored[c % 2], n * 48 + (16 + 16 * (c // 2)))
                nc.vector.tensor_tensor(osb[c % 2][rows, :], ps[rows, BG + c % 2, 0:HT],
                                        hres[rows, HT * (c % 2):HT * (c % 2) + HT], ALU.add)\
                    .then_inc(S["out_done"], 1)

            for part in range(3):
                softplus(0, part)
            cumsum(0)
            with dve.Fori(0, PAIRS) as i:
                for par in range(2):
                    n = i * 2 + par
                    for t in range(TILES):
                        k, d, j = t % 2, t // NJ, t % QJ
                        if t in (0, NJ):
                            dve.wait_ge(S["bc_done"], img("bc_done", n, 4 + 4 * d))
                        dve.wait_ge(T["u_bc"], tile(n, t))
                        dve.wait_ge(T["scan_done"], tile(n, t - 2))
                        nc.vector.tensor_tensor(two(dbx[k][:, :]), halves(BU), two(bcs[par][:, d, 0, :]), ALU.mult)\
                            .then_inc(T["dbx_done"], 1)
                        dve.wait_ge(T["da_done"], tile(n, t))
                        dve.wait_ge(T["dbx_done"], tile(n, t))
                        dve.wait_ge(T["ch_done"], tile(n, t - 2))
                        nc.vector.tensor_tensor_scan(hs[k][:, 0:TC], da[k][:, 0:TC], dbx[k][:, 0:TC], 0.0,
                                                     ALU.mult, ALU.add).then_inc(T["scan_done"], 1)
                        dve.wait_ge(T["scan_done"], tile(n, t))
                        dve.wait_ge(T["y_mm"], tile(n, t - 2))
                        nc.vector.tensor_tensor(ch[k][:, 0:TC], hs[k][:, 0:TC], bcs[par][:, d, 1, 0:TC], ALU.mult)\
                            .then_inc(T["ch_done"], 1)
                        dve.wait_ge(T["p_done"], tile(n, t))
                        dve.wait_ge(T["wdel_done"], tile(n, t - 2))
                        nc.vector.tensor_tensor(delta[:, k, 0:1], hs[k][:, NT:TC], hs[k][:, 0:1], ALU.subtract)\
                            .then_inc(T["del_done"], 1)
                        dve.wait_ge(T["del_done"], tile(n, t))
                        nc.vector.scalar_tensor_tensor(out=delta[:, k, 1:2], in0=pc[k][:, NT:TC],
                                                       scalar=delta[:, k, 0:1], in1=delta[:, k, 0:1],
                                                       op0=ALU.mult, op1=ALU.add).then_inc(T["del2_done"], 1)
                        dve.wait_ge(T["w_mm"], tile(n, t - 2))
                        dve.wait_ge(T["del2_done"], tile(n, t))
                        for c in range(2):
                            op = nc.vector.tensor_scalar(wdel[:, j, c, DB * j:DB * j + DB], w("mask8"),
                                                         delta[:, k, c:c + 1], None, ALU.mult)
                        op.then_inc(T["wdel_done"], 1)
                        if t == 0:
                            skip_add(n, 1 - par)
                        if 5 <= t < 8:
                            softplus(n + 1, t - 5)
                        if t == 7:
                            cumsum(n + 1)
                        if 13 <= t < 16:
                            for c in (2 * (t - 13), 2 * (t - 13) + 1):
                                add_residual(n, 1 - par, c)
            skip_add(B, 1)
            for c in range(6):
                add_residual(B, 1, c)


def experts(nc, ps, sem, w, w3, h2_d, out, selcb, v_eps):
    UNITS = PAIRS * NCK
    G = NTT * 2
    NQE = NE // 2
    STEPS = 2 * NE
    COUPLES = NCK // 2
    AHEAD = 3
    with ExitStack() as ctx:
        def sb(name, shape, dt=F32):
            return ctx.enter_context(nc.sbuf_tensor(name, shape, dt))

        hx, xn, res = ([sb(f"{n}{k}", [128, CK]) for k in range(NCK)] for n in ("hx", "xn", "res"))
        cen = [sb(f"cene{k}", [128, CK]) for k in range(4)]
        cparts = [sb(f"cparts{k}", [80, CK]) for k in range(4)]
        sq, osb = ([sb(f"{n}{k}", [128, CK]) for k in range(2)] for n in ("sqe", "oute"))
        var0 = sb("var0", [128, CK])
        lnv, rs = sb("lnve", [128, 2, CK]), sb("rse", [128, 2, CK])
        small = {n: sb("r_" + n, [TT, 2 * G, NE]) for n in
                 ("shift", "e", "key1", "sel1", "rest", "eq2", "key2", "sel2", "both", "num", "comb")}
        one = {n: sb("r1_" + n, [TT, 2 * G]) for n in ("mx", "k1", "m2", "k2", "den", "rden")}
        hid, scaled = ([sb(f"{n}{k}", [128, CK]) for k in range(4)] for n in ("hid", "hsc"))

        CHOOSE, ROUTE = 10, 4
        per_unit = dict(c_mm=1, sq=1, cen=1, v_mm=1, xn=1, res=1, tr_mm=1, cb_hi=1, cb_mid=1, cb_lo=1,
                        b_mm=8, h_mm=8, hid=8, scaled=8, l2_mm=NQE, o_done=1)
        per_couple = dict(var0=1, ln=2, rs=1, lg_mm=1, mx=1, shift=1, e=1, choose=CHOOSE, route=ROUTE)
        S = {n: sem("e_" + n) for n in {**per_unit, **per_couple}}
        hx_in = [sem(f"hx_in{k}") for k in range(NCK)]
        o_out = [sem(f"o_out{k}") for k in range(2)]
        ready = sem("e_ready")

        def unit(name, n, c):
            k = per_unit[name]
            return n * k + (NCK * k + c)

        def couple(name, n, c):
            k = per_couple[name]
            return n * k + (COUPLES * k + c)

        BC_, BV, BO, BB, BH = 0, 1, 2, 3, 5

        def bank(j, g):
            return BH + (STEPS * j + g) % AHEAD

        def since(j, g):
            loop = STEPS * COUPLES
            used = [BH + (at % loop) % AHEAD for at in range(-2 * AHEAD, STEPS * j + g + 1)]
            return 1 + used[-2::-1].index(used[-1])

        def hi(ap):
            return ap.bitcast(BF16)[..., 1::2]

        def wide(ap):
            return ap.unsqueeze(2).to_broadcast([TT, 2 * G, NE])

        block = ctx.enter_context(nc.Block())

        @block.sync
        def _(sp):
            for c in range(NCK):
                sp.dma_start(hx[c][:, :], h2_d[1, :, CK * c:CK * c + CK]).then_inc(hx_in[c], 16)
            with sp.Fori(0, PAIRS) as p:
                for c in range(NCK):
                    n = p * NCK + c
                    sp.wait_ge(S["res"], unit("res", n, 1))
                    sp.dma_start(hx[c][:, :], h2_d[p + 2, :, CK * c:CK * c + CK]).then_inc(hx_in[c], 16)
                    sp.wait_ge(S["o_done"], unit("o_done", n, 1))
                    sp.dma_start(out[p, :, CK * c:CK * c + CK], osb[c % 2][:, :]).then_inc(o_out[c % 2], 16)
            for k in range(NCK):
                sp.wait_ge(hx_in[k], 16 * (PAIRS + 1))
            for k in range(2):
                sp.wait_ge(o_out[k], 16 * (UNITS // 2 + 1))

        @block.gpsimd
        def _(pool):
            for n, k in per_unit.items():
                pool.sem_inc(S[n], NCK * k)
            for n, k in per_couple.items():
                pool.sem_inc(S[n], COUPLES * k)
            for k in range(2):
                pool.sem_inc(o_out[k], 16)
            for k in range(4):
                nc.gpsimd.memset(cparts[k][:, :], 0.0)
            nc.gpsimd.drain().then_inc(ready, 1)

            def normalize(m, k, cpl):
                pool.wait_ge(S["h_mm"], unit("h_mm", m - NCK, 8))
                pool.wait_ge(S["res"], unit("res", m - NCK, 1))
                pool.wait_ge(S["cen"], unit("cen", m, 1))
                pool.wait_ge(S["rs"], couple("rs", cpl, 1))
                nc.gpsimd.tensor_tensor(xn[k][:, :], cen[k % 4][:, :], rs[:, k % 2, :], ALU.mult).then_inc(S["xn"], 1)

            def residual(m, k, spread_to):
                pool.wait_ge(S["o_done"], unit("o_done", m - NCK, 1))
                pool.wait_ge(S["cb_lo"], unit("cb_lo", spread_to, 1))
                pool.wait_ge(S["xn"], unit("xn", m, 1))
                nc.gpsimd.tensor_tensor(res[k][:, :], hx[k][:, :], xn[k][:, :], ALU.add).then_inc(S["res"], 1)

            def spread(m, k, normalized):
                c = cparts[k % 4]
                pool.wait_ge(S["xn"], unit("xn", normalized, 1))
                pool.wait_ge(S["cb_lo"], unit("cb_lo", m, 0))
                pool.wait_ge(S["cb_mid"], unit("cb_mid", m, 1))
                nc.gpsimd.tensor_tensor(c[64:80, :], c[32:48, :], hi(c[32:48, :]), ALU.subtract).then_inc(S["cb_lo"], 1)

            def stages(c, j, first=False):
                m, k = c * 2 + 4, (2 * j + 4) % NCK
                for u in range(2):
                    normalize(m + u, k + u, c + 2)
                if not first:
                    for u in range(2):
                        spread(m - 2 + u, (k - 2 + u) % NCK, m + 1)
                for u in range(2):
                    residual(m + u, k + u, m - 1)

            stages(-2, -2, first=True)
            stages(-1, -1)
            with pool.Fori(0, PAIRS) as i:
                for j in range(COUPLES):
                    stages(i * COUPLES + j, j)

        @block.tensor
        def _(pe):
            def centre(m, k, loads):
                pe.wait_ge(hx_in[k], 16 * loads)
                pe.wait_ge(S["cen"], unit("cen", m, 0))
                nc.tensor.matmul(ps[:, BC_, 0:CK], w("cen"), hx[k][:, :], start=True, stop=True).then_inc(S["c_mm"], 1)

            def variance(m, k, cpl):
                if k % 2 == 0:
                    pe.wait_ge(S["shift"], couple("shift", cpl, 0))
                else:
                    pe.wait_ge(S["var0"], couple("var0", cpl, 1))
                pe.wait_ge(S["sq"], unit("sq", m, 1))
                nc.tensor.matmul(ps[:, BV, 0:CK], w("avg"), sq[k % 2][:, :], start=True, stop=True)\
                    .then_inc(S["v_mm"], 1)

            def logits(m, k):
                pe.wait_ge(S["xn"], unit("xn", m, 2))
                pe.wait_ge(S["cb_mid"], unit("cb_mid", m - 1, 1))
                for u in range(2):
                    for t in range(NTT):
                        at = NE * (G * u + 2 * t)
                        mm = nc.tensor.matmul(ps[0:TT, BV, at:at + 2 * NE], xn[k + u][:, TT * t:TT * t + TT],
                                              w("router"), start=True, stop=True)
                mm.then_inc(S["lg_mm"], 1)

            def turn(m, u, cpl):
                if u == 0:
                    pe.wait_ge(S["ln"], couple("ln", cpl + 1, 2))
                else:
                    pe.wait_ge(S["cb_mid"], unit("cb_mid", m, 0))
                pe.wait_ge(S["route"], couple("route", cpl, ROUTE))
                for t in range(NTT):
                    at = G * u + 2 * t
                    mm = nc.tensor.transpose(ps[0:2 * NE, BV, TT * t:TT * t + TT],
                                             small["comb"][:, at:at + 2, :].rearrange("p a b -> p (a b)"),
                                             w("ident"))
                mm.then_inc(S["tr_mm"], 1)

            def first(n, j, g):
                q, im, k = g % NE // 2, g % 2, 2 * j + g // NE
                rows = slice(64 * im, 64 * im + 64)
                pe.wait_ge(S["hid"], unit("hid", n, g + 1 - since(j, g)))
                nc.tensor.matmul(ps[:, bank(j, g), 0:CK], w3("ew1", 4)[rows, q, :], xn[k][rows, :],
                                 start=True, stop=True).then_inc(S["h_mm"], 1)

            def weights(n, j, g):
                q, im, k = g % NE // 2, g % 2, 2 * j + g // NE
                if g % NE == 0:
                    pe.wait_ge(S["cb_lo"], unit("cb_lo", n, 1 + g // NE))
                pe.wait_ge(S["scaled"], unit("scaled", n, g - 1))
                nc.tensor.matmul(ps[:, BB + im, 0:CK], selcb[:, NQE * im + q, :], hi(cparts[k % 4][:, :]),
                                 start=True, stop=True).then_inc(S["b_mm"], 1)

            def second(n, j, g):
                q, k = g % NE // 2, 2 * j + g // NE
                if q == 0:
                    pe.wait_ge(S["o_done"], unit("o_done", n, g // NE))
                    nc.tensor.matmul(ps[:, BO, 0:CK], w("eb2"), cparts[k % 4][0:2 * NE, :], start=True, stop=False)
                pe.wait_ge(S["scaled"], unit("scaled", n, g + 1))
                for im in range(2):
                    mm = nc.tensor.matmul(ps[64 * im:64 * im + 64, BO, 0:CK], w3("ew2", 4)[:, q, :],
                                          scaled[(2 * q + im) % 4][:, :], start=False, stop=(q == NQE - 1))
                mm.then_inc(S["l2_mm"], 1)

            pe.wait_ge(ready, 1)
            for c in range(3):
                if c == 2:
                    turn(0, 0, 0)
                    turn(1, 1, 0)
                if c > 0:
                    logits(2 * c - 2, 2 * c - 2)
                for u in range(2):
                    centre(2 * c + u, 2 * c + u, 1)
                    variance(2 * c + u, 2 * c + u, c)
            for g in range(AHEAD):
                first(0, 0, g)
            with pe.Fori(0, PAIRS) as i:
                for j in range(COUPLES):
                    c = i * COUPLES + j
                    n = i * NCK + 2 * j
                    k6 = 2 * j + 6
                    for g in range(STEPS):
                        weights(n, j, g)
                        if 1 <= g < STEPS - 2:
                            first(n, j, g + 2)
                        if g >= STEPS - 2:
                            first(n + 2, (j + 1) % COUPLES, g + 2 - STEPS)
                        if g in (2, 5):
                            turn(n + 2 + g // 4, g // 4, c + 1)
                        if g in (4, 7):
                            u = g // 6
                            centre(n + 6 + u, (k6 + u) % NCK, i + k6 // NCK + 1)
                        if g == 9:
                            logits(n + 4, (2 * j + 4) % NCK)
                        if g >= 3 and g % 2 == 1:
                            second(n, j, g - 2)
                        if g == 12:
                            variance(n + 6, 0, c + 3)
                        if g == 15:
                            variance(n + 7, 1, c + 3)
                    first(n + 2, (j + 1) % COUPLES, 2)
                    second(n, j, STEPS - 1)

        @block.scalar
        def _(act):
            def square(m, k):
                act.wait_ge(S["v_mm"], unit("v_mm", m - 1, 0))
                act.wait_ge(S["cen"], unit("cen", m, 1))
                nc.scalar.activation(sq[k % 2][:, :], cen[k % 4][:, :], ACT.Square).then_inc(S["sq"], 1)

            def keep_variance(m, cpl):
                act.wait_ge(S["ln"], couple("ln", cpl, 0))
                act.wait_ge(S["v_mm"], unit("v_mm", m, 1))
                nc.scalar.activation(var0[:, :], ps[:, BV, 0:CK], ACT.Copy).then_inc(S["var0"], 1)

            def log_variance(m, cpl):
                act.wait_ge(S["rs"], couple("rs", cpl, 0))
                act.wait_ge(S["var0"], couple("var0", cpl, 1))
                nc.scalar.activation(lnv[:, 0, :], var0[:, :], ACT.Ln, bias=v_eps).then_inc(S["ln"], 1)
                act.wait_ge(S["v_mm"], unit("v_mm", m, 2))
                nc.scalar.activation(lnv[:, 1, :], ps[:, BV, 0:CK], ACT.Ln, bias=v_eps).then_inc(S["ln"], 1)

            def norm(m, cpl):
                act.wait_ge(S["xn"], unit("xn", m, 0))
                act.wait_ge(S["ln"], couple("ln", cpl, 2))
                nc.scalar.activation(rs[:, :, :], lnv[:, :, :], ACT.Exp, scale=-0.5).then_inc(S["rs"], 1)

            def exponent(cpl):
                act.wait_ge(S["route"], couple("route", cpl, 0))
                act.wait_ge(S["shift"], couple("shift", cpl, 1))
                nc.scalar.activation(small["e"][:, :, :], small["shift"][:, :, :], ACT.Exp).then_inc(S["e"], 1)

            def gelu(n, j, g):
                act.wait_ge(S["scaled"], unit("scaled", n, g - 3))
                act.wait_ge(S["h_mm"], unit("h_mm", n, g + 1))
                q = g % NE // 2
                nc.scalar.activation(hid[g % 4][:, :], ps[:, bank(j, g), 0:CK], ACT.Gelu,
                                     bias=w("eb1")[:, q:q + 1]).then_inc(S["hid"], 1)

            act.wait_ge(ready, 1)
            nc.scalar.preload_act_table_set("natural_log_exp_and_others")
            for c in range(3):
                square(2 * c, 2 * c)
                keep_variance(2 * c, c)
                square(2 * c + 1, 2 * c + 1)
                if c < 2:
                    log_variance(2 * c, c)
                    norm(2 * c, c)
                if c == 1:
                    exponent(0)
            with act.Fori(0, PAIRS) as i:
                for j in range(COUPLES):
                    c = i * COUPLES + j
                    n = i * NCK + 2 * j
                    nc.scalar.preload_act_table_set("natural_log_exp_and_others")
                    log_variance(n + 4, c + 2)
                    exponent(c + 1)
                    norm(n + 4, c + 2)
                    for g in range(STEPS):
                        gelu(n, j, g)
                        if g == 8:
                            square(n + 6, 2 * j + 6)
                        if g == 11:
                            square(n + 7, 2 * j + 7)
                        if g == 13:
                            keep_variance(n + 6, c + 3)

        @block.vector
        def _(dve):
            s = {n: a[:, :, :] for n, a in small.items()}
            o = {n: a[:, :] for n, a in one.items()}
            rank = w("rank").rearrange("p (g e) -> p g e", e=NE)
            tt, v = nc.vector.tensor_tensor, nc.vector

            def keep_centred(m, k):
                dve.wait_ge(S["xn"], unit("xn", m - 4, 1))
                dve.wait_ge(S["c_mm"], unit("c_mm", m, 1))
                nc.vector.tensor_copy(cen[k % 4][:, :], ps[:, BC_, 0:CK]).then_inc(S["cen"], 1)

            def shift(cpl):
                lg = ps[0:TT, BV, 0:2 * G * NE].rearrange("p (g e) -> p g e", e=NE)
                dve.wait_ge(S["lg_mm"], couple("lg_mm", cpl, 1))
                v.tensor_reduce(o["mx"], lg, AX_X, ALU.max).then_inc(S["mx"], 1)
                dve.wait_ge(S["e"], couple("e", cpl, 0))
                dve.wait_ge(S["mx"], couple("mx", cpl, 1))
                tt(s["shift"], lg, wide(o["mx"]), ALU.subtract).then_inc(S["shift"], 1)

            def choose(cpl, part):
                def after(c):
                    dve.wait_ge(S["choose"], couple("choose", cpl, c))

                if part == 0:
                    dve.wait_ge(S["shift"], couple("shift", cpl, 1))
                    v.scalar_tensor_tensor(out=s["key1"], in0=s["shift"], scalar=0.0, in1=rank, op0=ALU.is_ge,
                                           op1=ALU.mult).then_inc(S["choose"], 1)
                    after(1)
                    v.tensor_reduce(o["k1"], s["key1"], AX_X, ALU.max).then_inc(S["choose"], 1)
                if part == 1:
                    after(2)
                    tt(s["sel1"], rank, wide(o["k1"]), ALU.is_equal).then_inc(S["choose"], 1)
                    after(3)
                    v.scalar_tensor_tensor(out=s["rest"], in0=s["sel1"], scalar=-3e38, in1=s["shift"], op0=ALU.mult,
                                           op1=ALU.add).then_inc(S["choose"], 1)
                if part == 2:
                    after(4)
                    v.tensor_reduce(o["m2"], s["rest"], AX_X, ALU.max).then_inc(S["choose"], 1)
                    after(5)
                    tt(s["eq2"], s["rest"], wide(o["m2"]), ALU.is_ge).then_inc(S["choose"], 1)
                if part == 3:
                    after(6)
                    tt(s["key2"], s["eq2"], rank, ALU.mult).then_inc(S["choose"], 1)
                    after(7)
                    v.tensor_reduce(o["k2"], s["key2"], AX_X, ALU.max).then_inc(S["choose"], 1)
                if part == 4:
                    after(8)
                    tt(s["sel2"], rank, wide(o["k2"]), ALU.is_equal).then_inc(S["choose"], 1)
                    dve.wait_ge(S["route"], couple("route", cpl, 0))
                    after(9)
                    tt(s["both"], s["sel1"], s["sel2"], ALU.add).then_inc(S["choose"], 1)

            def route(cpl, m):
                dve.wait_ge(S["choose"], couple("choose", cpl, CHOOSE))
                dve.wait_ge(S["e"], couple("e", cpl, 1))
                tt(s["num"], s["both"], s["e"], ALU.mult).then_inc(S["route"], 1)
                dve.wait_ge(S["route"], couple("route", cpl, 1))
                v.tensor_reduce(o["den"], s["num"], AX_X, ALU.add).then_inc(S["route"], 1)
                dve.wait_ge(S["route"], couple("route", cpl, 2))
                v.reciprocal(o["rden"], o["den"]).then_inc(S["route"], 1)
                dve.wait_ge(S["tr_mm"], unit("tr_mm", m, 0))
                dve.wait_ge(S["route"], couple("route", cpl, 3))
                tt(s["comb"], s["num"], wide(o["rden"]), ALU.mult).then_inc(S["route"], 1)

            def spread(m, k):
                dve.wait_ge(S["l2_mm"], unit("l2_mm", m - 4, NQE))
                dve.wait_ge(S["tr_mm"], unit("tr_mm", m, 1))
                c, tr = cparts[k % 4], ps[0:2 * NE, BV, 0:CK]
                nc.vector.tensor_copy(c[0:16, :], tr).then_inc(S["cb_hi"], 1)
                dve.wait_ge(S["cb_hi"], unit("cb_hi", m, 1))
                nc.vector.tensor_tensor(c[32:48, :], tr, hi(c[0:16, :]), ALU.subtract).then_inc(S["cb_mid"], 1)

            def finish(n, k, stores):
                dve.wait_ge(o_out[k % 2], 16 * stores)
                dve.wait_ge(S["res"], unit("res", n, 1))
                dve.wait_ge(S["l2_mm"], unit("l2_mm", n, NQE))
                nc.vector.tensor_tensor(osb[k % 2][:, :], ps[:, BO, 0:CK], res[k][:, :], ALU.add)\
                    .then_inc(S["o_done"], 1)

            def scale(n, g):
                dve.wait_ge(S["l2_mm"], unit("l2_mm", n, g // 2 - 1))
                dve.wait_ge(S["b_mm"], unit("b_mm", n, g + 1))
                dve.wait_ge(S["hid"], unit("hid", n, g + 1))
                nc.vector.tensor_tensor(scaled[g % 4][:, :], ps[:, BB + g % 2, 0:CK], hid[g % 4][:, :], ALU.mult)\
                    .then_inc(S["scaled"], 1)

            dve.wait_ge(ready, 1)
            for c in range(3):
                if c > 0:
                    if c == 2:
                        route(0, 0)
                        spread(0, 0)
                        spread(1, 1)
                    shift(c - 1)
                    for part in range(5):
                        choose(c - 1, part)
                keep_centred(2 * c, 2 * c)
                keep_centred(2 * c + 1, 2 * c + 1)
            with dve.Fori(0, PAIRS) as i:
                for j in range(COUPLES):
                    c = i * COUPLES + j
                    n = i * NCK + 2 * j
                    route(c + 1, n + 2)
                    for g in range(STEPS):
                        scale(n, g)
                        if g in (3, 6):
                            spread(n + 2 + g // 4, 2 * j + 2 + g // 4)
                        if g in (5, 8):
                            keep_centred(n + 6 + g // 8, 2 * j + 6 + g // 8)
                        if g == 9:
                            finish(n, 2 * j, i * COUPLES + (j + 1))
                        if g == 10:
                            shift(c + 2)
                        if g > 10:
                            choose(c + 2, g - 11)
                    finish(n + 1, 2 * j + 1, i * COUPLES + (j + 1))


def pack_weights(a):
    p = np.zeros((128, NW), np.float32)

    def put(name, v):
        at, rows, cols = AT[name]
        p[0:rows, at:at + cols] = np.asarray(v).reshape(rows, cols)

    t = lambda name: a["L0_tok_" + name]
    two = lambda v: np.concatenate([v, v])
    blk = lambda m: np.block([[m, np.zeros_like(m)], [np.zeros_like(m), m]])
    w1 = t("W1").reshape(2, KF, D)
    put("w1T", w1.transpose(2, 0, 1))
    put("w1dup", np.concatenate([w1, w1], axis=2).transpose(1, 0, 2))
    put("ln1g", t("ln1_g").reshape(2, KF).T)
    put("ln1b", t("ln1_b").reshape(2, KF).T)
    for name, key in (("b1", "b1"), ("g2", "ln2_g"), ("be2", "ln2_b"), ("bp1", "bp1"), ("gp", "lnp_g"),
                      ("bep", "lnp_b"), ("bp2", "bp2")):
        put(name, two(t(key)))
    put("wp1", blk(t("Wp1")))
    put("wp1T", blk(t("Wp1").T))
    put("wp2", blk(t("Wp2")))
    put("wp2T", blk(t("Wp2").T))
    put("cen", blk(np.eye(D, dtype=np.float32) - np.float32(1 / D)))
    put("avg", blk(np.full((D, D), 1 / D, np.float32)))
    put("ones1", np.full((KF, KF), 1 / NF, np.float32))
    m = lambda name: [a["L0_attn_f_" + name], a["L0_attn_r_" + name]]
    inw = m("in_w")
    put("inx", two(np.stack([v[0:D].T for v in inw], 1)))
    cw = np.stack([v[:, ::-1].T for v in m("conv_w")], 1)
    put("convw", np.repeat(cw, D, axis=0))
    inz = np.zeros((128, 2, D), np.float32)
    inz[0:D] = np.stack([v[D:2 * D].T for v in inw], 1)
    put("inz", inz)
    put("convb", np.concatenate(m("conv_b")))
    put("dtb", np.concatenate(m("dt_b")))
    put("dvec", np.concatenate(m("D")))
    put("wbc", np.concatenate([np.stack([np.concatenate([v[NR + NS * k:NR + NS * k + NS].T] * DB, 1)
                                         for k in range(2)], 1) for v in m("xproj_w")]))
    wdtr, wdt = np.zeros((128, 32), np.float32), np.zeros((32, 128), np.float32)
    for d in range(2):
        wdtr[D * d:D * d + D, NR * d:NR * d + NR] = m("xproj_w")[d][0:NR].T
        wdt[NR * d:NR * d + NR, D * d:D * d + D] = m("dt_w")[d].T
    put("wdtr", wdtr)
    put("wdt", wdt)
    put("alog", np.stack([v.reshape(NJ, DB * NS) for v in m("A_log")]).reshape(TILES, 128).T)
    wout = np.zeros((128, 2, D), np.float32)
    for d in range(2):
        wout[D * d:D * d + D, d] = m("out_w")[d].T
    put("wout", wout)
    ch = np.arange(128) // NS
    ysel = np.zeros((128, QJ, 32), np.float32)
    selbc = np.zeros((3, 32, QJ, 128), np.float32)
    for j in range(QJ):
        ysel[np.arange(128), j, DB * j + ch] = 1
        selbc[:, DB * j + ch, j, np.arange(128)] = 1
    put("ysel", ysel)
    put("selbc", selbc)
    put("mask8", ch[:, None] == np.arange(DB)[None, :])
    f = lambda name: a["L0_ffn_" + name]
    put("router", blk(f("router_w").T))
    put("ew1", two(f("w1").reshape(4, 2, D, D).transpose(2, 0, 1, 3).reshape(D, 4 * 128)))
    put("eb1", f("b1").reshape(4, 128).T)
    put("ew2", f("w2").reshape(4, 128, D).transpose(1, 0, 2))
    eb2 = np.zeros((2, NE, 2, D), np.float32)
    selcb = np.zeros((80, 2, 4, 128), np.float32)
    for im in range(2):
        eb2[im, :, im] = f("b2")
        for e in range(4):
            for part in range(3):
                for k in range(2):
                    selcb[32 * part + NE * im + 2 * e + k, im, e, D * k:D * k + D] = 1
    put("eb2", eb2)
    put("selcb", selcb)
    put("rank", np.broadcast_to(np.arange(NE, 0, -1, dtype=np.float32), (TT, NTT * 4, NE)))
    put("ident", np.eye(TT, dtype=np.float32))
    return p


def kernel(**inputs):
    import numpy as _np
    import concourse.bacc as _bacc
    from concourse import mybir as _mybir
    from concourse.bass_utils import run_bass_kernel_spmd as _run

    a = {k: _np.asarray(v) for k, v in inputs.items()}
    g = IMG // PATCH
    x = a["x"].reshape(PAIRS, 2, CH, g, PATCH, g, PATCH).transpose(0, 4, 6, 2, 1, 3, 5)
    x = x.reshape(PAIRS, 2, KF, 2, 2, HT).transpose(0, 4, 2, 1, 3, 5)
    nc = _bacc.Bacc("TRN2", target_bir_lowering=False, num_devices=1)
    arrays = {"x_dram": _np.ascontiguousarray(x.reshape(PAIRS, 2, KF, 2, 2 * HT)), "w_dram": pack_weights(a)}
    args = [nc.dram_tensor(n, v.shape, _mybir.dt.from_np(v.dtype), kind="ExternalInput").ap()
            for n, v in arrays.items()]
    out = nc.dram_tensor("out_dram", (PAIRS, 128, L), F32, kind="ExternalOutput").ap()
    vit_tower(nc, *args, out)
    r = _run(nc, [arrays], core_ids=[0])
    got = r.results[0]["out_dram"]
    return _np.ascontiguousarray(got.reshape(B, D, L).transpose(0, 2, 1))
```
